# Optimizing a Trainium2 kernel written in Bass

```python
import numpy as np
import jax
import jax.numpy as jnp

def _softmax(x, axis=-1):
    return jax.nn.softmax(x, axis=axis)

def _gelu(x):
    return jax.nn.gelu(x, approximate=True)

def _silu(x):
    return jax.nn.silu(x)

def _sigmoid(x):
    return jax.nn.sigmoid(x)

def _layernorm(x, axis=-1, eps=1e-05):
    m = jnp.mean(x, axis=axis, keepdims=True)
    v = jnp.var(x, axis=axis, keepdims=True)
    return (x - m) / jnp.sqrt(v + eps)

def _scatter_add(tgt, idx, src, axis=0):
    return tgt.at[idx].add(src)

def _segment_sum(src, seg, n):
    return jax.ops.segment_sum(src, seg, n)
kernel_name = 'mk_xattn_seq_d2_seqx_r4_e37ab4'

def setup_inputs(seed: int=0):
    np.random.seed(seed)
    _w = jnp.asarray

    def _rec_inputs():
        import jax
        import jax.numpy as jnp
        _rk = jax.random.key(seed)
        x = 7.22e-05 + 1 * jax.random.normal(jax.random.fold_in(_rk, 1), (32, 128, 512), jnp.float32)
        _lenS = 128 - jax.random.randint(jax.random.fold_in(_rk, 7), (32,), 0, max(1, 128 // 4) + 1, jnp.int32)
        _lenS2 = 128 - jax.random.randint(jax.random.fold_in(_rk, 8), (32,), 0, max(1, 128 // 4) + 1, jnp.int32)
        _ctx_2048P = jax.random.normal(jax.random.fold_in(_rk, 11), (32, 16, 512), jnp.float32)
        _ctx_2048c = jax.random.dirichlet(jax.random.fold_in(_rk, 511), 0.3 * jnp.ones((16,), jnp.float32), (32, 128))
        _ctx_2048t = jnp.einsum('bsk,bkd->bsd', _ctx_2048c, _ctx_2048P)
        _ctx_2048t = _ctx_2048t * jax.lax.rsqrt(jnp.mean(jnp.square(_ctx_2048t)) + 1e-12) * 0.953939
        ctx_2048 = 4.13588e-05 + 0.999923 * (_ctx_2048t + 0.3 * jax.random.normal(jax.random.fold_in(_rk, 611), (32, 128, 512), jnp.float32))
        _validS = jnp.arange(128)[None, :] < _lenS[:, None]
        _validS2 = jnp.arange(128)[None, :] < _lenS2[:, None]
        _causal = jnp.tril(jnp.ones((128, 128), dtype=bool))
        mask_Bx1xSxS2_ff0 = jnp.where(jnp.ones((32, 1, 128, 128), dtype=bool), 0.0, -1000000000.0).astype(jnp.float32)
        return (x, ctx_2048, mask_Bx1xSxS2_ff0)
    x, ctx_2048, mask_Bx1xSxS2_ff0 = _rec_inputs()

    def _L0_xattn_setup():
        import jax, jax.numpy as jnp
        import numpy as np
        B, C, N = (8, 128, 512)
        key = jax.random.key(seed)
        ks = jax.random.split(key, 7)
        s = 1.0 / np.sqrt(C)
        return {'x': jax.random.normal(ks[0], (B, C, N), dtype=jnp.float32), 'y': jax.random.normal(ks[1], (B, C, N), dtype=jnp.float32), 'w_qk': jax.random.normal(ks[2], (C, C), dtype=jnp.float32) * s, 'w_v': jax.random.normal(ks[3], (C, C), dtype=jnp.float32) * s, 'b_v': jax.random.normal(ks[4], (C,), dtype=jnp.float32) * s, 'w_t': jax.random.normal(ks[5], (C, C), dtype=jnp.float32) * s, 'b_t': jax.random.normal(ks[6], (C,), dtype=jnp.float32) * s}
    _L0_xattn_all = _L0_xattn_setup()
    _L0_xattn_in = {k: v for k, v in _L0_xattn_all.items() if k in ('w_qk', 'w_v', 'b_v', 'w_t', 'b_t')}
    del _L0_xattn_all

    def _L1_xattn_setup():
        import jax, jax.numpy as jnp
        import numpy as np
        H = 512
        NH = 32
        KVH = 8
        HD = H // NH
        GROUPS = NH // KVH
        EPS = 1e-06
        B, L, S = (4, 256, 256)

        def _gqa_forward(hidden_state, encoder_hidden_state, encoder_attention_mask, Wq, bq, Wk, bk, Wv, bv, Wo, bo, gamma, beta):
            b, l, _ = hidden_state.shape
            s = encoder_hidden_state.shape[1]
            q = hidden_state @ Wq + bq
            k = encoder_hidden_state @ Wk + bk
            v = encoder_hidden_state @ Wv + bv
            q = q.reshape(b, l, KVH, GROUPS, HD).transpose(0, 2, 3, 1, 4)
            k = k.reshape(b, s, KVH, HD).transpose(0, 2, 1, 3)
            v = v.reshape(b, s, KVH, HD).transpose(0, 2, 1, 3)
            scale = 1.0 / jnp.sqrt(jnp.asarray(HD, q.dtype))
            scores = jnp.einsum('bkgld,bksd->bkgls', q, k) * scale
            scores = scores + encoder_attention_mask[:, :, None, :, :]
            attn = jax.nn.softmax(scores, axis=-1)
            out = jnp.einsum('bkgls,bksd->bkgld', attn, v)
            out = out.transpose(0, 3, 1, 2, 4).reshape(b, l, H)
            out = out @ Wo + bo
            x = out + hidden_state
            mu = jnp.mean(x, axis=-1, keepdims=True)
            var = jnp.var(x, axis=-1, keepdims=True)
            return (x - mu) * jax.lax.rsqrt(var + EPS) * gamma + beta
        key = jax.random.key(seed)
        ks = jax.random.split(key, 12)
        sd = 0.02
        return {'hidden_state': jax.random.normal(ks[0], (B, L, H), jnp.float32), 'encoder_hidden_state': jax.random.normal(ks[1], (B, S, H), jnp.float32), 'encoder_attention_mask': jnp.zeros((B, 1, L, S), jnp.float32), 'Wq': jax.random.normal(ks[2], (H, H), jnp.float32) * sd, 'bq': jnp.zeros((H,), jnp.float32), 'Wk': jax.random.normal(ks[3], (H, KVH * HD), jnp.float32) * sd, 'bk': jnp.zeros((KVH * HD,), jnp.float32), 'Wv': jax.random.normal(ks[4], (H, KVH * HD), jnp.float32) * sd, 'bv': jnp.zeros((KVH * HD,), jnp.float32), 'Wo': jax.random.normal(ks[5], (H, H), jnp.float32) * sd, 'bo': jnp.zeros((H,), jnp.float32), 'gamma': jnp.ones((H,), jnp.float32), 'beta': jnp.zeros((H,), jnp.float32)}
    _L1_xattn_all = _L1_xattn_setup()
    _L1_xattn_in = {k: v for k, v in _L1_xattn_all.items() if k in ('Wq', 'bq', 'Wk', 'bk', 'Wv', 'bv', 'Wo', 'bo', 'gamma', 'beta')}
    del _L1_xattn_all
    return {'x': x, 'ctx_2048': ctx_2048, 'mask_Bx1xSxS2_ff0': mask_Bx1xSxS2_ff0, 'L0_xattn_w_qk': _L0_xattn_in['w_qk'], 'L0_xattn_w_v': _L0_xattn_in['w_v'], 'L0_xattn_b_v': _L0_xattn_in['b_v'], 'L0_xattn_w_t': _L0_xattn_in['w_t'], 'L0_xattn_b_t': _L0_xattn_in['b_t'], 'L1_xattn_Wq': _L1_xattn_in['Wq'], 'L1_xattn_bq': _L1_xattn_in['bq'], 'L1_xattn_Wk': _L1_xattn_in['Wk'], 'L1_xattn_bk': _L1_xattn_in['bk'], 'L1_xattn_Wv': _L1_xattn_in['Wv'], 'L1_xattn_bv': _L1_xattn_in['bv'], 'L1_xattn_Wo': _L1_xattn_in['Wo'], 'L1_xattn_bo': _L1_xattn_in['bo'], 'L1_xattn_gamma': _L1_xattn_in['gamma'], 'L1_xattn_beta': _L1_xattn_in['beta']}

def reference(x, ctx_2048, mask_Bx1xSxS2_ff0, L0_xattn_w_qk, L0_xattn_w_v, L0_xattn_b_v, L0_xattn_w_t, L0_xattn_b_t, L1_xattn_Wq, L1_xattn_bq, L1_xattn_Wk, L1_xattn_bk, L1_xattn_Wv, L1_xattn_bv, L1_xattn_Wo, L1_xattn_bo, L1_xattn_gamma, L1_xattn_beta):
    import jax
    import jax.numpy as jnp

    def _L0_xattn_ref(x, y, w_qk, w_v, b_v, w_t, b_t):
        import jax, jax.numpy as jnp
        import numpy as np
        B, C, N = (8, 128, 512)
        x_q = jnp.einsum('oc,bcn->bno', w_qk, y)
        x_k = jnp.einsum('oc,bcn->bon', w_qk, x)
        x_v = jnp.einsum('oc,bcn->bon', w_v, x) + b_v[None, :, None]
        energy = jnp.einsum('bnc,bcm->bnm', x_q, x_k)
        attention = jax.nn.softmax(energy, axis=-1)
        attention = attention / (1e-07 + attention.sum(axis=1, keepdims=True))
        x_r = jnp.einsum('bcn,bnm->bcm', x_v, attention)
        x_r = jax.nn.relu(jnp.einsum('oc,bcn->bon', w_t, x - x_r) + b_t[None, :, None])
        return x + x_r

    def _L1_xattn_ref(hidden_state, encoder_hidden_state, encoder_attention_mask, Wq, bq, Wk, bk, Wv, bv, Wo, bo, gamma, beta):
        import jax, jax.numpy as jnp
        import numpy as np
        H = 512
        NH = 32
        KVH = 8
        HD = H // NH
        GROUPS = NH // KVH
        EPS = 1e-06
        B, L, S = (4, 256, 256)

        def _gqa_forward(hidden_state, encoder_hidden_state, encoder_attention_mask, Wq, bq, Wk, bk, Wv, bv, Wo, bo, gamma, beta):
            b, l, _ = hidden_state.shape
            s = encoder_hidden_state.shape[1]
            q = hidden_state @ Wq + bq
            k = encoder_hidden_state @ Wk + bk
            v = encoder_hidden_state @ Wv + bv
            q = q.reshape(b, l, KVH, GROUPS, HD).transpose(0, 2, 3, 1, 4)
            k = k.reshape(b, s, KVH, HD).transpose(0, 2, 1, 3)
            v = v.reshape(b, s, KVH, HD).transpose(0, 2, 1, 3)
            scale = 1.0 / jnp.sqrt(jnp.asarray(HD, q.dtype))
            scores = jnp.einsum('bkgld,bksd->bkgls', q, k) * scale
            scores = scores + encoder_attention_mask[:, :, None, :, :]
            attn = jax.nn.softmax(scores, axis=-1)
            out = jnp.einsum('bkgls,bksd->bkgld', attn, v)
            out = out.transpose(0, 3, 1, 2, 4).reshape(b, l, H)
            out = out @ Wo + bo
            x = out + hidden_state
            mu = jnp.mean(x, axis=-1, keepdims=True)
            var = jnp.var(x, axis=-1, keepdims=True)
            return (x - mu) * jax.lax.rsqrt(var + EPS) * gamma + beta
        return _gqa_forward(hidden_state, encoder_hidden_state, encoder_attention_mask, Wq, bq, Wk, bk, Wv, bv, Wo, bo, gamma, beta)
    x = _L0_xattn_ref(x, ctx_2048, L0_xattn_w_qk, L0_xattn_w_v, L0_xattn_b_v, L0_xattn_w_t, L0_xattn_b_t)
    x = _L1_xattn_ref(x, ctx_2048, mask_Bx1xSxS2_ff0, L1_xattn_Wq, L1_xattn_bq, L1_xattn_Wk, L1_xattn_bk, L1_xattn_Wv, L1_xattn_bv, L1_xattn_Wo, L1_xattn_bo, L1_xattn_gamma, L1_xattn_beta)
    return x

_drawn_inputs = setup_inputs


def setup_inputs(seed=0):
    import zlib

    import numpy as np

    out = dict(_drawn_inputs(seed))
    spreads = {'L1_xattn_bq': (0.0, 0.8),
     'L1_xattn_bk': (0.0, 0.8),
     'L1_xattn_bv': (0.0, 0.1),
     'L1_xattn_bo': (0.0, 0.1),
     'L1_xattn_gamma': (1.0, 0.2),
     'L1_xattn_beta': (0.0, 0.1)}
    factors = {'L1_xattn_Wq': 6.779, 'L1_xattn_Wk': 6.684}
    for name, (base, spread) in spreads.items():
        noise = np.random.default_rng([zlib.crc32(name.encode()), seed]).standard_normal(out[name].shape)
        drawn = base * np.exp(spread * noise) if base else spread * noise
        out[name] = jnp.asarray(drawn.astype(out[name].dtype))
    for name, factor in factors.items():
        out[name] = (out[name] * factor).astype(out[name].dtype)
    return out
```

```python
from contextlib import ExitStack

import numpy as np

import concourse.bass as bass
from concourse import mybir

F32 = mybir.dt.float32
F32R = mybir.dt.float32r
I32 = mybir.dt.int32
ALU = mybir.AluOpType
ACT = mybir.ActivationFunctionType
AX = mybir.AxisListType

P = 128
B = 32
PAIRS = B // 2
N = 512
KC = N // P
KV = 8
G = 4
HD = 16
SCALE = 0.25
COL_EPS = 1e-7
LN_EPS = 1e-6

ONE = P
A0 = P + 2
X0 = A0 + P
CW = X0 + P
BW = P + 2

C_ID = 0
C_KVMASK = C_ID + P
C_ONES = C_KVMASK + KV
C_GMASK = C_ONES + 2 * 2 * HD
C_SEL = C_GMASK + G * P
C_ALL = C_SEL + KV

GEN_USES = (
    [(f"z{j}", 1) for j in range(2)]
    + [(f"tva{j}{k}", 1) for j in range(2) for k in range(KC)]
    + [(f"q{g}", 2) for g in range(G)]
    + [("r0", 2), ("r1", 2), ("m0", 2), ("m1", 2)]
    + [("et0", 1), ("et1", 1), ("wo0", 2), ("k", 1), ("v", 1), ("vt0", 1), ("vt1", 1), ("wo1", 2)]
)
WIDE_USES = (
    [("mx00", 2), ("mx01", 2), ("en00", 1), ("mx02", 2), ("en01", 1), ("mx03", 2), ("en10", 1), ("en11", 1)]
    + [("st00", 2), ("mx10", 2), ("st01", 2), ("mx11", 2), ("st02", 2), ("mx12", 2), ("st03", 2), ("mx13", 2)]
    + [("st10", 2), ("st11", 2), ("st12", 2), ("st13", 2), ("b0", 1), ("b1", 1)]
)


def ring(uses, stages, stages_before):
    now = [n for n, s in uses if s in stages]
    before = [n for n, s in uses if s in stages_before]
    assert len(now) % 2 == 0 and len(before) % 2 == 0
    plan = {}
    for at, name in enumerate(now):
        if at >= 2:
            plan[name] = (at % 2, now[at - 2], 0)
        elif before:
            plan[name] = (at % 2, before[len(before) - 2 + at], 1)
        else:
            plan[name] = (at % 2, None, 0)
    return plan


def build_xattn(nc, x, ctx, mask, w_qk, w_v, w_t, b_t, Wq, Wk, Wv, Wo, bo, gamma, beta, columns, consts, out):
    es = ExitStack()
    with es:
        def sb(name, shape, dt=F32):
            return es.enter_context(nc.sbuf_tensor(name, shape, dt))

        def ps(name, shape):
            return es.enter_context(nc.psum_tensor(name, shape, F32))

        cst = sb("cst", [P, C_ALL])
        ident = cst[:, C_ID:C_ID + P]
        kvmask = cst[:, C_KVMASK:C_KVMASK + KV]
        ones_eo = cst[:, C_ONES:C_ONES + 4 * HD].rearrange("p (o c) -> p o c", o=2)
        gmask = cst[0:32, C_GMASK:C_GMASK + G * P]
        sel_f = cst[0:32, C_SEL:C_SEL + KV]
        sel = sb("sel", [32, KV], F32R)
        ident4 = sb("ident4", [P, G, P], F32R)
        cols = sb("cols", [P, G + 3])
        bq_raw, bk_s, bv_s, b0_s = cols[:, 0:G], cols[:, G:G + 1], cols[:, G + 1:G + 2], cols[:, G + 2:G + 3]
        gram_h = sb("gram_h", [P, P], F32R)
        gram_l = sb("gram_l", [P, P], F32R)
        cw_h = sb("cw_h", [P, CW], F32R)
        cw_l = sb("cw_l", [P, CW], F32R)
        cb_s = sb("cb_s", [P, CW])
        att = sb("att", [P, 2, KC, N])
        setup = att[:].rearrange("p a b n -> p (a b n)")
        stage_kv = setup[:, 0:2 * N].rearrange("p (w k c) -> p w k c", w=2, k=KC)
        cw_s = setup[:, 4 * N:4 * N + CW]
        wqk_s, wv_s, wt_s, wtT_s = (setup[:, 5 * N + n * P:5 * N + (n + 1) * P] for n in range(4))
        late = sb("late", [P, 4, 2, N])
        stage_w = late[:, 0:2].rearrange("p a b n -> p (a b) n")
        wtmp = late[:, 2:4].rearrange("p a b n -> p (a b) n")
        wq_h = sb("wq_h", [P, KC, G, P], F32R)
        wq_l = sb("wq_l", [P, KC, G, P], F32R)
        wkv_h = sb("wkv_h", [P, 2, KC, P], F32R)
        wkv_l = sb("wkv_l", [P, 2, KC, P], F32R)
        wo_h = sb("wo_h", [P, G, N], F32R)
        wo_l = sb("wo_l", [P, G, N], F32R)
        bq_s = sb("bq_s", [P, G])
        bo_b = sb("bo_b", [P, N])
        gamma_b = sb("gamma_b", [P, N])
        beta_b = sb("beta_b", [P, N])
        flag_col = sb("flag_col", [P, 1])
        flag_i = sb("flag_i", [1, 1], I32)

        xs = sb("xs", [P, 2, N])
        ys = sb("ys", [P, 2, N])
        mk = sb("mk", [P, 2, P])
        xh = sb("xh", [P, 2, N], F32R)
        xl = sb("xl", [P, 2, N], F32R)
        yh = sb("yh", [P, 2, N], F32R)
        yl = sb("yl", [P, 2, N], F32R)
        zh = sb("zh", [P, 2, N], F32R)
        zl = sb("zl", [P, 2, N], F32R)
        ta = sb("ta", [P, 2, KC, CW])
        negmax = sb("negmax", [P, 2, KC])
        rowsum = sb("rowsum", [P, 2, KC])
        rowinv = sb("rowinv", [P, 2, KC])
        colneg = sb("colneg", [P, 2, KC])
        colinv = sb("colinv", [P, 2, KC])
        x2 = sb("x2", [P, KC, 2, P])
        x2h = sb("x2h", [P, KC, 2, P], F32R)
        x2l = sb("x2l", [P, KC, 2, P], F32R)
        eth = sb("eth", [P, KC, 2, P], F32R)
        etl = sb("etl", [P, KC, 2, P], F32R)
        kh = sb("kh", [P, 2, P], F32R)
        kl = sb("kl", [P, 2, P], F32R)
        kbh = sb("kbh", [P, 2, KV, P], F32R)
        kbl = sb("kbl", [P, 2, KV, P], F32R)
        vts = sb("vts", [P, 2, P])
        v2 = sb("v2", [P, 2, KV, 2 * HD])
        qh = sb("qh", [P, 2, G, P], F32R)
        ql = sb("ql", [P, 2, G, P], F32R)
        mrow = sb("mrow", [P, 2, G * KV], F32R)
        mrep = sb("mrep", [32, G * P], F32R)
        prob = sb("prob", [P, KV, G * P])
        stage_o = prob[:, 0:G]
        at, xr, res, outb = (late[:, n] for n in range(4))
        ath = sb("ath", [P, G, P], F32R)
        atl = sb("atl", [P, G, P], F32R)
        bns = sb("bns", [P, 2, 6])
        mv = sb("mv", [P, 2, 2])
        nv = sb("nv", [P, 2, 8])
        yi = sb("yi", [P, 2, 1], I32)

        wide = ps("wide", [P, 2, 2, N])
        gen = ps("gen", [P, 2, N])
        den = ps("den", [P, N])
        outt = ps("outt", [P, N])

        SEMS = dict(
            xh_done=2, x_split=2, yh_done=2, y_split=2, kb_done=4, xrb_done=2, gam_done=2, out_ready=2,
            z_ps=2, tva_ps=8, et_ps=2, k_ps=1, v_ps=1, vt_ps=2, en_ps=8, b_ps=2,
            q_ps=4, r_ps=2, mx_ps=8, m_ps=2, st_ps=8, den_ps=2, o_ps=2, wo_ps=2,
            zh_done=2, exp_done=8, tv_done=8, eth_done=2, kh_done=1, vts_done=1, v2_done=4, x2h_done=2,
            qh_done=4, xr_done=2, prob_done=8, ath_done=2, nrm_done=2,
            zl_done=2, ta_done=8, negmax_done=8, rowinv_done=2, colneg_done=2, colinv_done=2, pre_done=8,
            x2_done=2, x2l_done=2, etl_done=2, kl_done=1, ql_done=4, mrow_done=8, mrep_done=2, dinv_done=2,
            at_done=2, atl_done=2, res_done=2, bns_done=2, newton=22,
        )
        sem = {k: es.enter_context(nc.semaphore(k)) for k in SEMS}
        x_in = es.enter_context(nc.semaphore("x_in"))
        y_in = es.enter_context(nc.semaphore("y_in"))
        mask_in = es.enter_context(nc.semaphore("mask_in"))
        out_sem = [es.enter_context(nc.semaphore(f"out_done{j}")) for j in range(2)]
        w0_in = es.enter_context(nc.semaphore("w0_in"))
        w1_in = es.enter_context(nc.semaphore("w1_in"))
        allmask_in = es.enter_context(nc.semaphore("allmask_in"))
        setup_pe = es.enter_context(nc.semaphore("setup_pe"))
        setup_dve = es.enter_context(nc.semaphore("setup_dve"))
        cw_ready = es.enter_context(nc.semaphore("cw_ready"))
        weights_ready = es.enter_context(nc.semaphore("weights_ready"))
        flag_ps = es.enter_context(nc.semaphore("flag_ps"))
        flag_ready = es.enter_context(nc.semaphore("flag_ready"))
        zeros_ready = es.enter_context(nc.semaphore("zeros_ready"))

        def wait(eng, name, pair, n):
            value = pair * SEMS[name] + (n + 1)
            if isinstance(value, int) and value <= 0:
                return
            eng.wait_ge(sem[name], value)

        RELEASE = {}
        for j in range(2):
            RELEASE[f"z{j}"] = ("zl_done", j, 1)
            RELEASE[f"et{j}"] = ("etl_done", j, 1)
            RELEASE[f"vt{j}"] = ("v2_done", 2 * j + 1, 1)
            RELEASE[f"r{j}"] = ("xr_done", j, 2)
            RELEASE[f"m{j}"] = ("mrep_done", j, 2)
            RELEASE[f"wo{j}"] = ("res_done", j, 2)
            RELEASE[f"b{j}"] = ("pre_done", 4 * j + 3, 1)
            for k in range(4):
                RELEASE[f"tva{j}{k}"] = ("ta_done", 4 * j + k, 1)
                RELEASE[f"mx{j}{k}"] = ("mrow_done", 4 * j + k, 2)
                RELEASE[f"st{j}{k}"] = ("prob_done", 4 * j + k, 2)
            for h in range(2):
                RELEASE[f"en{j}{h}"] = ("exp_done", 4 * j + 2 * h + 1, 1)
        for g in range(G):
            RELEASE[f"q{g}"] = ("ql_done", g, 2)
        RELEASE["k"] = ("kl_done", 0, 1)
        RELEASE["v"] = ("vts_done", 0, 1)

        def plans(stages, before):
            return {**ring(GEN_USES, stages, before), **ring(WIDE_USES, stages, before)}

        def slot(plan, name):
            return plan[name][0]

        def wait_slot(eng, plan, name, i):
            _, prev, back = plan[name]
            if prev is not None:
                signal, n, stage = RELEASE[prev]
                wait(eng, signal, i - back - (1 if stage == 2 else 0), n)

        FIRST, SECOND, FULL, LAST = (
            plans((1,), ()), plans((1, 2), (1,)), plans((1, 2), (1, 2)), plans((2,), (1, 2)))

        block = es.enter_context(nc.Block())

        @block.sync
        def _(sp):
            def load_x(pair):
                sp.dma_start(xs[:], x[bass.ts(pair, 2)].rearrange("b c n -> c b n")).then_inc(x_in, 16)

            def load_y(pair):
                sp.dma_start(ys[:], ctx[bass.ts(pair, 2)].rearrange("b c n -> c b n")).then_inc(y_in, 16)

            def load_mask(pair):
                sp.dma_start(mk[:], mask[bass.ts(pair, 2)].rearrange("b o l s -> l (b o) s")).then_inc(mask_in, 16)

            def store(pair, j):
                sp.dma_start(out[bass.ds(pair * 2 + j, 1)].rearrange("b l h -> l b h"),
                             outb[:, j:j + 1, :]).then_inc(out_sem[j], 16)

            def iteration(i, load_next, s1, s2):
                if load_next:
                    wait(sp, "x_split", i, 1)
                    load_x(i + 1)
                    wait(sp, "y_split", i, 1)
                    wait(sp, "et_ps", i, 1)
                    load_y(i + 1)
                if s1:
                    if not isinstance(i, int) or i > 0:
                        sp.wait_ge(mask_in, i * 16)
                    wait(sp, "st_ps", i - 1, 7)
                    load_mask(i)
                if s2:
                    for j in range(2):
                        wait(sp, "out_ready", i - 1, j)
                        store(i - 1, j)

            load_x(0)
            load_y(0)
            for dst, src in ((cst[:], consts), (wqk_s, w_qk), (wv_s, w_v), (wt_s, w_t),
                             (cols[:], columns),
                             (cb_s[:, A0:A0 + P], b_t.partition_broadcast(P))):
                sp.dma_start(dst, src).then_inc(w0_in, 16)
            sp.dma_start(stage_kv[:, 0], Wk.rearrange("(k p) n -> p k n", p=P)).then_inc(w0_in, 16)
            sp.dma_start(stage_kv[:, 1], Wv.rearrange("(k p) n -> p k n", p=P)).then_inc(w0_in, 16)
            sp.dma_start(stage_w, Wq.rearrange("(k p) n -> p k n", p=P)).then_inc(w1_in, 16)
            sp.dma_start(bo_b[:], bo.partition_broadcast(P)).then_inc(w1_in, 16)
            sp.dma_start(gamma_b[:], gamma.partition_broadcast(P)).then_inc(w1_in, 16)
            sp.dma_start(beta_b[:], beta.partition_broadcast(P)).then_inc(w1_in, 16)
            sp.dma_start(prob[:].rearrange("p k n -> p (k n)"),
                         mask.rearrange("b o l s -> (b o l s)").rearrange("(p f) -> p f", p=P)
                         ).then_inc(allmask_in, 16)
            iteration(0, True, True, False)
            sp.wait_ge(setup_dve, 5)
            sp.dma_start(stage_o, Wo.rearrange("(g p) n -> p g n", g=G)).then_inc(w1_in, 16)

            iteration(1, True, True, True)
            with sp.Fori(2, PAIRS - 1) as i:
                iteration(i, True, True, True)
            iteration(PAIRS - 1, False, True, True)
            iteration(PAIRS, False, False, True)
            for j in range(2):
                sp.wait_ge(out_sem[j], 16 * PAIRS)

        @block.gpsimd
        def _(pool):
            one_col = ones_eo[:, 0, 0:1].broadcast_to([P, N])
            nc.gpsimd.memset(v2[:], 0.0).then_inc(zeros_ready, 1)

            def split_x(i, j):
                if j == 0:
                    pool.wait_ge(x_in, i * 16 + 16)
                wait(pool, "tva_ps", i - 1, 4 * j + 3)
                nc.gpsimd.tensor_tensor(xh[:, j], xs[:, j], one_col, ALU.mult).then_inc(sem["xh_done"], 1)
                wait(pool, "xh_done", i, j)
                nc.gpsimd.tensor_tensor(xl[:, j], xs[:, j], xh[:, j].bitcast(F32), ALU.subtract
                                        ).then_inc(sem["x_split"], 1)

            def split_y(i, j):
                if j == 0:
                    pool.wait_ge(y_in, i * 16 + 16)
                wait(pool, "en_ps", i - 1, 4 * j + 3)
                nc.gpsimd.tensor_tensor(yh[:, j], ys[:, j], one_col, ALU.mult).then_inc(sem["yh_done"], 1)
                wait(pool, "yh_done", i, j)
                nc.gpsimd.tensor_tensor(yl[:, j], ys[:, j], yh[:, j].bitcast(F32), ALU.subtract
                                        ).then_inc(sem["y_split"], 1)

            def spread_k(i, j):
                if j == 0:
                    wait(pool, "kl_done", i, 0)
                    wait(pool, "st_ps", i - 1, 7)
                shape = [P, KV, P]
                for src, dst in ((kh, kbh), (kl, kbl)):
                    nc.gpsimd.tensor_tensor(dst[:, j], src[:, j].bitcast(F32).unsqueeze(1).broadcast_to(shape),
                                            kvmask.unsqueeze(2).broadcast_to(shape), ALU.mult
                                            ).then_inc(sem["kb_done"], 1)

            def residual_bias(q, j):
                wait(pool, "xr_done", q, j)
                nc.gpsimd.tensor_tensor(xr[:, j], xr[:, j], bo_b[:], ALU.add).then_inc(sem["xrb_done"], 1)

            def scale_shift(q, j):
                wait(pool, "nrm_done", q, j)
                store_before = q * 16
                if not isinstance(store_before, int) or store_before > 0:
                    pool.wait_ge(out_sem[j], store_before)
                nc.gpsimd.tensor_tensor(outb[:, j], res[:, j], gamma_b[:], ALU.mult).then_inc(sem["gam_done"], 1)
                wait(pool, "gam_done", q, j)
                nc.gpsimd.tensor_tensor(outb[:, j], outb[:, j], beta_b[:], ALU.add).then_inc(sem["out_ready"], 1)

            def iteration(i, s1, s2):
                if s1:
                    split_x(i, 0)
                    split_x(i, 1)
                    split_y(i, 0)
                    split_y(i, 1)
                if s2:
                    residual_bias(i - 1, 0)
                    residual_bias(i - 1, 1)
                if s2:
                    scale_shift(i - 1, 0)
                if s1:
                    spread_k(i, 0)
                    spread_k(i, 1)
                if s2:
                    scale_shift(i - 1, 1)

            pool.wait_ge(w0_in, 16 * 8)
            iteration(0, True, False)
            pool.wait_ge(w1_in, 16 * 5)
            iteration(1, True, True)
            with pool.Fori(2, PAIRS) as i:
                iteration(i, True, True)
            iteration(PAIRS, False, True)

        @block.tensor
        def _(pe):
            mm = nc.tensor.matmul

            pe.wait_ge(w0_in, 16 * 8)
            mm(gen[:, 0, 0:P], wqk_s, wqk_s, start=True, stop=True)
            nc.tensor.transpose(den[:, 0:P], wt_s, ident).then_inc(setup_pe, 1)
            pe.wait_ge(setup_dve, 2)
            mm(gen[:, 1, 0:P], wv_s, wtT_s, start=True, stop=True)
            mm(outt[:, 0:P], b0_s.broadcast_to([P, P]), wtT_s, start=True, stop=True).then_inc(setup_pe, 1)
            pe.wait_ge(cw_ready, 1)

            def z_project(i, plan, j):
                wait(pe, "x_split", i, j)
                wait_slot(pe, plan, f"z{j}", i)
                o = gen[:, slot(plan, f"z{j}")]
                mm(o, gram_h[:], xh[:, j], start=True, stop=False)
                mm(o, gram_h[:], xl[:, j], start=False, stop=False)
                mm(o, gram_l[:], xh[:, j], start=False, stop=True).then_inc(sem["z_ps"], 1)

            def tva_project(i, plan, j, k):
                name = f"tva{j}{k}"
                wait_slot(pe, plan, name, i)
                o = gen[:, slot(plan, name)]
                a, b = xh[:, j, bass.ts(k, P)], xl[:, j, bass.ts(k, P)]
                mm(o[:, 0:CW], a, cw_h[:], start=True, stop=False)
                mm(o[:, 0:CW], b, cw_h[:], start=False, stop=False)
                mm(o[:, 0:X0], a, cw_l[:, 0:X0], start=False, stop=True).then_inc(sem["tva_ps"], 1)

            def energy(i, plan, j, h):
                name = f"en{j}{h}"
                wait(pe, "zl_done", i, j)
                wait(pe, "y_split", i, j)
                wait_slot(pe, plan, name, i)
                for n in range(2 * h, 2 * h + 2):
                    o = wide[:, slot(plan, name), n % 2]
                    a, b = yh[:, j, bass.ts(n, P)], yl[:, j, bass.ts(n, P)]
                    mm(o, a, zh[:, j], start=True, stop=False)
                    mm(o, a, zl[:, j], start=False, stop=False)
                    mm(o, b, zh[:, j], start=False, stop=True).then_inc(sem["en_ps"], 1)

            def attend(i, plan, j):
                name = f"b{j}"
                wait(pe, "tv_done", i, 4 * j + 3)
                wait_slot(pe, plan, name, i)
                for m in range(KC):
                    o = wide[:, slot(plan, name), m // 2, (m % 2) * 256:(m % 2) * 256 + BW]
                    for n in range(KC):
                        last = mm(o, att[:, j, n, bass.ts(m, P)], ta[:, j, n, 0:BW], start=n == 0, stop=n == KC - 1)
                last.then_inc(sem["b_ps"], 1)

            def ctx_transpose(i, plan, j):
                name = f"et{j}"
                if j == 0:
                    pe.wait_ge(y_in, i * 16 + 16)
                wait_slot(pe, plan, name, i)
                for k in range(KC):
                    last = nc.tensor.transpose(gen[:, slot(plan, name), bass.ts(k, P)], ys[:, j, bass.ts(k, P)], ident)
                last.then_inc(sem["et_ps"], 1)

            def kv_project(i, plan, name, n, done):
                wait(pe, "etl_done", i, 1)
                wait_slot(pe, plan, name, i)
                o = gen[:, slot(plan, name), 0:2 * P]
                for k in range(KC):
                    mm(o, wkv_h[:, n, k], eth[:, k], start=k == 0, stop=False)
                    mm(o, wkv_h[:, n, k], etl[:, k], start=False, stop=False)
                    last = mm(o, wkv_l[:, n, k], eth[:, k], start=False, stop=k == KC - 1)
                last.then_inc(sem[done], 1)

            def v_transpose(i, plan, j):
                name = f"vt{j}"
                wait(pe, "vts_done", i, 0)
                wait_slot(pe, plan, name, i)
                nc.tensor.transpose(gen[:, slot(plan, name), 0:P], vts[:, j], ident).then_inc(sem["vt_ps"], 1)

            def q_project(q, plan, i, g):
                name = f"q{g}"
                if g == 0:
                    wait(pe, "x2l_done", q, 1)
                wait_slot(pe, plan, name, i)
                o = gen[:, slot(plan, name), 0:2 * P]
                for k in range(KC):
                    mm(o, wq_h[:, k, g], x2h[:, k], start=k == 0, stop=False)
                    mm(o, wq_h[:, k, g], x2l[:, k], start=False, stop=False)
                    last = mm(o, wq_l[:, k, g], x2h[:, k], start=False, stop=k == KC - 1)
                last.then_inc(sem["q_ps"], 1)

            def residual_transpose(q, plan, i, j):
                name = f"r{j}"
                wait(pe, "x2_done", q, j)
                wait_slot(pe, plan, name, i)
                for k in range(KC):
                    last = nc.tensor.transpose(gen[:, slot(plan, name), bass.ts(k, P)], x2[:, k, j], ident)
                last.then_inc(sem["r_ps"], 1)

            def max_scores(q, plan, i, j, g, masked):
                name = f"mx{j}{g}"
                wait(pe, "ql_done", q, g)
                wait(pe, "kb_done", q, 2 * j + 1)
                wait_slot(pe, plan, name, i)
                for half in range(2):
                    o = wide[:, slot(plan, name), half]
                    last = mm(o, qh[:, j, g], kbh[:, j, 4 * half:4 * half + 4], start=True, stop=not masked)
                    if masked:
                        last = mm(o, ident, mk[:, j].unsqueeze(1).broadcast_to([P, 4, P]), start=False, stop=True)
                last.then_inc(sem["mx_ps"], 1)

            def max_spread(q, plan, i, j):
                name = f"m{j}"
                wait(pe, "mrow_done", q, 4 * j + 3)
                wait_slot(pe, plan, name, i)
                mm(gen[0:32, slot(plan, name)], mrow[:, j], ident4[:], start=True, stop=True).then_inc(sem["m_ps"], 1)

            def scores(q, plan, i, j, p, masked):
                name = f"st{j}{p}"
                wait(pe, "mrep_done", q, j)
                wait_slot(pe, plan, name, i)
                for half in range(2):
                    kv = 2 * p + half
                    o = wide[:, slot(plan, name), half]
                    mm(o, kbh[:, j, kv], qh[:, j], start=True, stop=False)
                    mm(o, kbh[:, j, kv], ql[:, j], start=False, stop=False)
                    mm(o, kbl[:, j, kv], qh[:, j], start=False, stop=False)
                    last = mm(o, sel[:, kv:kv + 1].broadcast_to([32, P]), mrep[:], start=False, stop=not masked)
                    if masked:
                        last = mm(o, mk[:, j], ident.unsqueeze(1).broadcast_to([P, G, P]), start=False, stop=True)
                last.then_inc(sem["st_ps"], 1)

            def weigh(q, j, dst, operand, done):
                wait(pe, "prob_done", q, 4 * j + 3)
                wait(pe, "at_done", q, j - 1)
                for odd in range(2):
                    for p in range(KV // 2):
                        last = mm(dst[32 * p:32 * p + 32, :], operand(2 * p + odd, odd), prob[:, 2 * p + odd],
                                  start=odd == 0, stop=odd == 1, tile_position=(0, 32 * p))
                last.then_inc(sem[done], 1)

            def denominators(q, j):
                weigh(q, j, den, lambda kv, odd: ones_eo[:, odd], "den_ps")

            def values(q, j):
                if j == 0:
                    wait(pe, "v2_done", q, 3)
                weigh(q, j, outt, lambda kv, odd: v2[:, j, kv], "o_ps")

            def out_project(q, plan, i, j):
                name = f"wo{j}"
                wait(pe, "atl_done", q, j)
                wait_slot(pe, plan, name, i)
                o = gen[:, slot(plan, name)]
                for g in range(G):
                    mm(o, ath[:, g], wo_h[:, g], start=g == 0, stop=False)
                    mm(o, ath[:, g], wo_l[:, g], start=False, stop=False)
                    last = mm(o, atl[:, g], wo_h[:, g], start=False, stop=g == G - 1)
                last.then_inc(sem["wo_ps"], 1)

            def iteration(i, plan, s1, s2, masked):
                q = i - 1
                if s1:
                    z_project(i, plan, 0)
                    z_project(i, plan, 1)
                    for j in range(2):
                        for k in range(KC):
                            tva_project(i, plan, j, k)
                if s2:
                    for g in range(G):
                        q_project(q, plan, i, g)
                    residual_transpose(q, plan, i, 0)
                    residual_transpose(q, plan, i, 1)
                    max_scores(q, plan, i, 0, 0, masked)
                    max_scores(q, plan, i, 0, 1, masked)
                if s1:
                    energy(i, plan, 0, 0)
                if s2:
                    max_scores(q, plan, i, 0, 2, masked)
                if s1:
                    energy(i, plan, 0, 1)
                if s2:
                    max_scores(q, plan, i, 0, 3, masked)
                if s1:
                    energy(i, plan, 1, 0)
                if s2:
                    max_spread(q, plan, i, 0)
                if s1:
                    energy(i, plan, 1, 1)
                if s2:
                    for p in range(4):
                        scores(q, plan, i, 0, p, masked)
                        max_scores(q, plan, i, 1, p, masked)
                    denominators(q, 0)
                    max_spread(q, plan, i, 1)
                    values(q, 0)
                    for p in range(4):
                        scores(q, plan, i, 1, p, masked)
                if s1:
                    ctx_transpose(i, plan, 0)
                    ctx_transpose(i, plan, 1)
                if s2:
                    out_project(q, plan, i, 0)
                if s1:
                    kv_project(i, plan, "k", 0, "k_ps")
                    kv_project(i, plan, "v", 1, "v_ps")
                if s2:
                    denominators(q, 1)
                    values(q, 1)
                if s1:
                    v_transpose(i, plan, 0)
                    v_transpose(i, plan, 1)
                    attend(i, plan, 0)
                    attend(i, plan, 1)
                if s2:
                    out_project(q, plan, i, 1)

            iteration(0, FIRST, True, False, False)
            pe.wait_ge(setup_dve, 5)
            mm(den[0:1, 0:1], flag_col[:], ones_eo[:, 0, 0:1], start=True, stop=True).then_inc(flag_ps, 1)
            pe.wait_ge(weights_ready, 1)
            pe.wait_ge(flag_ready, 1)
            any_mask = pe.value_load(flag_i[0:1, 0:1], min_val=0, max_val=1)

            def rest(masked):
                if masked:
                    pe.wait_ge(mask_in, 16)
                iteration(1, SECOND, True, True, masked)
                with pe.Fori(2, PAIRS) as i:
                    if masked:
                        pe.wait_ge(mask_in, i * 16)
                    iteration(i, FULL, True, True, masked)
                if masked:
                    pe.wait_ge(mask_in, PAIRS * 16)
                iteration(PAIRS, LAST, False, True, masked)

            with pe.If(any_mask > 0):
                rest(True)
            with pe.Else():
                rest(False)

        @block.scalar
        def _(act):
            ident_f, copy_f, exp_f = ACT.Identity, ACT.Copy, ACT.Exp

            def z_high(i, plan, j):
                wait(act, "z_ps", i, j)
                wait(act, "en_ps", i - 1, 4 * j + 3)
                nc.scalar.activation(zh[:, j], gen[:, slot(plan, f"z{j}")], copy_f).then_inc(sem["zh_done"], 1)

            def exp_energy(i, plan, j, n):
                wait(act, "negmax_done", i, 4 * j + n)
                wait(act, "b_ps", i - 1, j)
                nc.scalar.activation(att[:, j, n], wide[:, slot(plan, f"en{j}{n // 2}"), n % 2], exp_f,
                                     bias=negmax[:, j, n:n + 1], accum_out=rowsum[:, j, n:n + 1]
                                     ).then_inc(sem["exp_done"], 1)

            def scale_values(i, j):
                wait(act, "rowinv_done", i, j)
                for n in range(KC):
                    nc.scalar.activation(ta[:, j, n, 0:BW], ta[:, j, n, 0:BW], copy_f,
                                         scale=rowinv[:, j, n:n + 1]).then_inc(sem["tv_done"], 1)

            def ctx_high(i, plan, j):
                wait(act, "et_ps", i, j)
                wait(act, "v_ps", i - 1, 0)
                nc.scalar.activation(eth[:, :, j], gen[:, slot(plan, f"et{j}")].rearrange("p (k s) -> p k s", k=KC),
                                     copy_f).then_inc(sem["eth_done"], 1)

            def k_high(i, plan):
                wait(act, "k_ps", i, 0)
                wait(act, "kb_done", i - 1, 3)
                nc.scalar.activation(kh[:], gen[:, slot(plan, "k"), 0:2 * P].rearrange("p (j s) -> p j s", j=2),
                                     ident_f, bias=bk_s).then_inc(sem["kh_done"], 1)

            def v_biased(i, plan):
                wait(act, "v_ps", i, 0)
                wait(act, "vt_ps", i - 1, 1)
                nc.scalar.activation(vts[:], gen[:, slot(plan, "v"), 0:2 * P].rearrange("p (j s) -> p j s", j=2),
                                     ident_f, bias=bv_s).then_inc(sem["vts_done"], 1)

            def v_place(i, plan, j):
                wait(act, "vt_ps", i, j)
                wait(act, "o_ps", i - 1, 1)
                src = gen[:, slot(plan, f"vt{j}"), 0:P].rearrange("p (k o d) -> p k o d", o=2, d=HD)
                dst = v2[:, j].rearrange("p (k o) c -> p k o c", o=2)
                for odd in range(2):
                    nc.scalar.activation(dst[:, :, odd, HD * odd:HD * odd + HD], src[:, :, odd], copy_f
                                         ).then_inc(sem["v2_done"], 1)

            def x2_high(i, j):
                wait(act, "x2_done", i, j)
                wait(act, "q_ps", i - 1, 3)
                nc.scalar.activation(x2h[:, :, j], x2[:, :, j], copy_f).then_inc(sem["x2h_done"], 1)

            def q_high(q, plan, g):
                wait(act, "q_ps", q, g)
                wait(act, "st_ps", q - 1, 7)
                nc.scalar.activation(qh[:, :, g], gen[:, slot(plan, f"q{g}"), 0:2 * P].rearrange("p (j l) -> p j l", j=2),
                                     ident_f, bias=bq_s[:, g:g + 1]).then_inc(sem["qh_done"], 1)

            def residual(q, plan, j):
                wait(act, "r_ps", q, j)
                wait(act, "res_done", q - 1, j)
                nc.scalar.activation(xr[:, j], gen[:, slot(plan, f"r{j}")], copy_f).then_inc(sem["xr_done"], 1)

            def exp_scores(q, plan, j, p):
                wait(act, "st_ps", q, 4 * j + p)
                wait(act, "o_ps", q, j - 1)
                nc.scalar.activation(prob[:, 2 * p:2 * p + 2], wide[:, slot(plan, f"st{j}{p}")], exp_f
                                     ).then_inc(sem["prob_done"], 1)

            def at_high(q, j):
                wait(act, "at_done", q, j)
                wait(act, "wo_ps", q, j - 1)
                nc.scalar.activation(ath[:], at[:, j].rearrange("p (g l) -> p g l", g=G), copy_f
                                     ).then_inc(sem["ath_done"], 1)

            def normalise(q, j):
                wait(act, "newton", q, 11 * j + 10)
                nc.scalar.activation(res[:, j], res[:, j], ident_f, bias=nv[:, j, 7:8], scale=nv[:, j, 6:7]
                                     ).then_inc(sem["nrm_done"], 1)

            def iteration(i, plan, s1, s2):
                q = i - 1
                if s1:
                    z_high(i, plan, 0)
                    z_high(i, plan, 1)
                if s2:
                    for g in range(G):
                        q_high(q, plan, g)
                    residual(q, plan, 0)
                    residual(q, plan, 1)
                if s1:
                    for j in range(2):
                        for n in range(KC):
                            exp_energy(i, plan, j, n)
                if s2:
                    exp_scores(q, plan, 0, 0)
                    exp_scores(q, plan, 0, 1)
                if s1:
                    scale_values(i, 0)
                    scale_values(i, 1)
                if s2:
                    exp_scores(q, plan, 0, 2)
                    exp_scores(q, plan, 0, 3)
                    for p in range(4):
                        exp_scores(q, plan, 1, p)
                    at_high(q, 0)
                if s1:
                    ctx_high(i, plan, 0)
                    ctx_high(i, plan, 1)
                    k_high(i, plan)
                if s2:
                    normalise(q, 0)
                if s1:
                    v_biased(i, plan)
                    v_place(i, plan, 0)
                    v_place(i, plan, 1)
                if s2:
                    at_high(q, 1)
                if s1:
                    x2_high(i, 0)
                    x2_high(i, 1)
                if s2:
                    normalise(q, 1)

            act.wait_ge(w0_in, 16 * 8)
            act.wait_ge(zeros_ready, 1)
            iteration(0, FIRST, True, False)
            act.wait_ge(weights_ready, 1)
            iteration(1, SECOND, True, True)
            with act.Fori(2, PAIRS) as i:
                iteration(i, FULL, True, True)
            iteration(PAIRS, LAST, False, True)

        @block.vector
        def _(dve):
            tt, stt, cp = nc.vector.tensor_tensor, nc.vector.scalar_tensor_tensor, nc.vector.tensor_copy

            dve.wait_ge(w0_in, 16 * 8)
            nc.vector.memset(cw_s[:, ONE:A0], 0.0)
            nc.vector.memset(cb_s[:, ONE:ONE + 1], 1.0)
            nc.vector.memset(cb_s[:, ONE + 1:ONE + 2], 0.0)
            nc.vector.memset(cb_s[:, X0:CW], 0.0)
            cp(cw_s[:, X0:CW], ident)
            cp(sel[:], sel_f)
            cp(ident4[:], ident.unsqueeze(1).broadcast_to([P, G, P]))
            dve.wait_ge(setup_pe, 1)
            cp(gram_h[:], gen[:, 0, 0:P]).then_inc(setup_dve, 1)
            cp(wtT_s, den[:, 0:P]).then_inc(setup_dve, 1)
            dve.wait_ge(setup_dve, 1)
            tt(gram_l[:], gen[:, 0, 0:P], gram_h[:].bitcast(F32), ALU.subtract)
            cp(cw_s[:, A0:X0], den[:, 0:P])
            dve.wait_ge(setup_pe, 2)
            cp(cb_s[:, 0:P], outt[:, 0:P])
            cp(cw_s[:, 0:P], gen[:, 1, 0:P]).then_inc(setup_dve, 1)
            dve.wait_ge(setup_dve, 3)
            cp(cw_h[:], cw_s)
            cp(wkv_h[:], stage_kv[:]).then_inc(setup_dve, 1)
            dve.wait_ge(setup_dve, 4)
            tt(wkv_l[:], stage_kv, wkv_h[:].bitcast(F32), ALU.subtract)
            tt(cw_l[:], cw_s, cw_h[:].bitcast(F32), ALU.subtract).then_inc(cw_ready, 1)

            def setup_mask_flag():
                dve.wait_ge(allmask_in, 16)
                masks = prob[:].rearrange("p k n -> p (k n)")
                nc.vector.tensor_scalar(masks, masks, 0.0, None, ALU.not_equal).then_inc(flag_ready_dve, 1)
                dve.wait_ge(flag_ready_dve, 1)
                nc.vector.tensor_reduce(flag_col[:], masks, AX.X, ALU.max).then_inc(setup_dve, 1)

            def setup_flag_value():
                dve.wait_ge(flag_ps, 1)
                nc.vector.tensor_scalar(flag_i[:], den[0:1, 0:1], 1.0, None, ALU.min).then_inc(flag_ready, 1)

            def setup_weights():
                dve.wait_ge(w1_in, 16 * 5)
                nc.vector.tensor_scalar(bq_s[:], bq_raw, SCALE, None, ALU.mult)
                last = nc.vector.tensor_scalar(wtmp, stage_w, SCALE, None, ALU.mult)
                last.then_inc(wsplit, 1)
                dve.wait_ge(wsplit, 1)
                cp(wq_h[:].rearrange("p k g c -> p k (g c)"), wtmp)
                cp(wo_h[:], stage_o).then_inc(wsplit, 1)
                dve.wait_ge(wsplit, 2)
                tt(wq_l[:].rearrange("p k g c -> p k (g c)"), wtmp,
                   wq_h[:].bitcast(F32).rearrange("p k g c -> p k (g c)"), ALU.subtract)
                tt(wo_l[:], stage_o, wo_h[:].bitcast(F32), ALU.subtract).then_inc(weights_ready, 1)

            flag_ready_dve = es.enter_context(nc.semaphore("flag_marks"))
            wsplit = es.enter_context(nc.semaphore("wsplit"))

            def z_low(i, plan, j):
                wait(dve, "zh_done", i, j)
                wait(dve, "en_ps", i - 1, 4 * j + 3)
                tt(zl[:, j], gen[:, slot(plan, f"z{j}")], zh[:, j].bitcast(F32), ALU.subtract
                   ).then_inc(sem["zl_done"], 1)

            def tva_out(i, plan, j, k):
                wait(dve, "tva_ps", i, 4 * j + k)
                wait(dve, "b_ps", i - 1, j)
                wait(dve, "x2_done", i - 1, j)
                tt(ta[:, j, k], gen[:, slot(plan, f"tva{j}{k}"), 0:CW], cb_s[:], ALU.add
                   ).then_inc(sem["ta_done"], 1)

            def energy_max(i, plan, j, n):
                wait(dve, "en_ps", i, 4 * j + n)
                wait(dve, "exp_done", i - 1, 4 * j + n)
                nc.vector.tensor_reduce(negmax[:, j, n:n + 1], wide[:, slot(plan, f"en{j}{n // 2}"), n % 2],
                                        AX.X, ALU.max, negate=True).then_inc(sem["negmax_done"], 1)

            def row_inverse(i, j):
                wait(dve, "exp_done", i, 4 * j + 3)
                wait(dve, "tv_done", i - 1, 4 * j + 3)
                nc.vector.reciprocal(rowinv[:, j], rowsum[:, j]).then_inc(sem["rowinv_done"], 1)

            def layer0_out(i, plan, j):
                wait(dve, "b_ps", i, j)
                att_v = wide[:, slot(plan, f"b{j}")].rearrange("p a (b c) -> p (a b) c", b=2)
                nc.vector.tensor_scalar(colneg[:, j], att_v[:, :, ONE], -1.0, -COL_EPS, ALU.mult, ALU.add
                                        ).then_inc(sem["colneg_done"], 1)
                wait(dve, "colneg_done", i, j)
                nc.vector.reciprocal(colinv[:, j], colneg[:, j]).then_inc(sem["colinv_done"], 1)
                wait(dve, "colinv_done", i, j)
                for m in range(KC):
                    stt(ta[:, j, m, A0:A0 + P], att_v[:, m, 0:P], colinv[:, j, m:m + 1], ta[:, j, m, A0:A0 + P],
                        ALU.mult, ALU.add).then_inc(sem["pre_done"], 1)
                wait(dve, "pre_done", i, 4 * j + 3)
                wait(dve, "x2l_done", i - 1, j)
                wait(dve, "r_ps", i - 1, j)
                stt(x2[:, :, j], ta[:, j, :, A0:A0 + P], 0.0, ta[:, j, :, X0:CW], ALU.max, ALU.add
                    ).then_inc(sem["x2_done"], 1)

            def x2_low(i, j):
                wait(dve, "x2h_done", i, j)
                wait(dve, "q_ps", i - 1, 3)
                tt(x2l[:, :, j], x2[:, :, j], x2h[:, :, j].bitcast(F32), ALU.subtract).then_inc(sem["x2l_done"], 1)

            def ctx_low(i, plan, j):
                wait(dve, "eth_done", i, j)
                wait(dve, "v_ps", i - 1, 0)
                tt(etl[:, :, j], gen[:, slot(plan, f"et{j}")].rearrange("p (k s) -> p k s", k=KC),
                   eth[:, :, j].bitcast(F32), ALU.subtract).then_inc(sem["etl_done"], 1)

            def k_low(i, plan):
                wait(dve, "kh_done", i, 0)
                wait(dve, "kb_done", i - 1, 3)
                stt(kl[:], gen[:, slot(plan, "k"), 0:2 * P].rearrange("p (j s) -> p j s", j=2), bk_s,
                    kh[:].bitcast(F32), ALU.add, ALU.subtract).then_inc(sem["kl_done"], 1)

            def q_low(q, plan, g):
                wait(dve, "qh_done", q, g)
                wait(dve, "st_ps", q - 1, 7)
                stt(ql[:, :, g], gen[:, slot(plan, f"q{g}"), 0:2 * P].rearrange("p (j l) -> p j l", j=2),
                    bq_s[:, g:g + 1], qh[:, :, g].bitcast(F32), ALU.add, ALU.subtract).then_inc(sem["ql_done"], 1)

            def score_max(q, plan, j, g):
                wait(dve, "mx_ps", q, 4 * j + g)
                wait(dve, "m_ps", q - 1, j)
                nc.vector.tensor_reduce(mrow[:, j, bass.ts(g, KV)],
                                        wide[:, slot(plan, f"mx{j}{g}")].rearrange("p a (b s) -> p (a b) s", s=P),
                                        AX.X, ALU.max, negate=True).then_inc(sem["mrow_done"], 1)

            def max_rows(q, plan, j):
                wait(dve, "m_ps", q, j)
                wait(dve, "st_ps", q, 4 * j - 1)
                tt(mrep[:], gen[0:32, slot(plan, f"m{j}")], gmask, ALU.mult).then_inc(sem["mrep_done"], 1)

            def weigh_out(q, j):
                wait(dve, "den_ps", q, j)
                wait(dve, "atl_done", q - 1, j)
                nc.vector.reciprocal(at[:, j], den[:]).then_inc(sem["dinv_done"], 1)
                wait(dve, "dinv_done", q, j)
                wait(dve, "o_ps", q, j)
                tt(at[:, j], outt[:], at[:, j], ALU.mult).then_inc(sem["at_done"], 1)

            def at_low(q, j):
                wait(dve, "ath_done", q, j)
                wait(dve, "wo_ps", q, j - 1)
                tt(atl[:], at[:, j].rearrange("p (g l) -> p g l", g=G), ath[:].bitcast(F32), ALU.subtract
                   ).then_inc(sem["atl_done"], 1)

            def layernorm_stats(q, plan, j):
                wait(dve, "wo_ps", q, j)
                wait(dve, "xrb_done", q, j)
                wait(dve, "gam_done", q - 1, j)
                tt(res[:, j], gen[:, slot(plan, f"wo{j}")], xr[:, j], ALU.add).then_inc(sem["res_done"], 1)
                wait(dve, "res_done", q, j)
                nc.vector.bn_stats(bns[:, j], res[:, j]).then_inc(sem["bns_done"], 1)
                wait(dve, "bns_done", q, j)
                step = [0]

                def link(ins):
                    ins.then_inc(sem["newton"], 1)
                    wait(dve, "newton", q, 11 * j + step[0])
                    step[0] += 1

                v, half, y, y1, t, dev = (nv[:, j, c:c + 1] for c in range(6))
                rstd, shift = nv[:, j, 6:7], nv[:, j, 7:8]
                tt(mv[:, j], bns[:, j, 1:3], bns[:, j, 4:6], ALU.add)
                link(tt(dev, bns[:, j, 1:2], bns[:, j, 4:5], ALU.subtract))
                nc.vector.tensor_scalar(t, mv[:, j, 1:2], 1.0 / N, LN_EPS, ALU.mult, ALU.add)
                link(stt(y1, dev, 0.25, dev, ALU.mult, ALU.mult))
                link(tt(v, t, y1, ALU.add))
                nc.vector.tensor_scalar(half, v, -0.5, None, ALU.mult)
                link(nc.vector.tensor_scalar(yi[:, j], v.bitcast(I32), -0.5, 1597463007.0, ALU.mult, ALU.add))
                y0 = yi[:, j].bitcast(F32)
                link(stt(t, y0, half, y0, ALU.mult, ALU.mult))
                link(stt(y, t, 1.5, y0, ALU.add, ALU.mult))
                link(stt(t, y, half, y, ALU.mult, ALU.mult))
                link(stt(y1, t, 1.5, y, ALU.add, ALU.mult))
                link(stt(t, y1, half, y1, ALU.mult, ALU.mult))
                link(stt(rstd, t, 1.5, y1, ALU.add, ALU.mult))
                link(nc.vector.tensor_scalar(shift, mv[:, j, 0:1], rstd, -0.5, ALU.mult, ALU.mult))

            def iteration(i, plan, s1, s2):
                q = i - 1
                if s1:
                    z_low(i, plan, 0)
                    z_low(i, plan, 1)
                    for j in range(2):
                        for k in range(KC):
                            tva_out(i, plan, j, k)
                if s2:
                    for g in range(G):
                        q_low(q, plan, g)
                    score_max(q, plan, 0, 0)
                    score_max(q, plan, 0, 1)
                if s1:
                    energy_max(i, plan, 0, 0)
                    energy_max(i, plan, 0, 1)
                if s2:
                    score_max(q, plan, 0, 2)
                if s1:
                    energy_max(i, plan, 0, 2)
                    energy_max(i, plan, 0, 3)
                if s2:
                    score_max(q, plan, 0, 3)
                if s1:
                    energy_max(i, plan, 1, 0)
                    energy_max(i, plan, 1, 1)
                if s2:
                    max_rows(q, plan, 0)
                if s1:
                    energy_max(i, plan, 1, 2)
                    energy_max(i, plan, 1, 3)
                    row_inverse(i, 0)
                if s2:
                    score_max(q, plan, 1, 0)
                if s1:
                    row_inverse(i, 1)
                if s2:
                    for g in range(1, G):
                        score_max(q, plan, 1, g)
                    max_rows(q, plan, 1)
                    weigh_out(q, 0)
                    at_low(q, 0)
                if s1:
                    ctx_low(i, plan, 0)
                    ctx_low(i, plan, 1)
                if s2:
                    layernorm_stats(q, plan, 0)
                if s1:
                    k_low(i, plan)
                if s2:
                    weigh_out(q, 1)
                    at_low(q, 1)
                if s1:
                    layer0_out(i, plan, 0)
                    layer0_out(i, plan, 1)
                    x2_low(i, 0)
                    x2_low(i, 1)
                if s2:
                    layernorm_stats(q, plan, 1)

            iteration(0, FIRST, True, False)
            setup_mask_flag()
            setup_flag_value()
            setup_weights()
            iteration(1, SECOND, True, True)
            with dve.Fori(2, PAIRS) as i:
                iteration(i, FULL, True, True)
            iteration(PAIRS, LAST, False, True)


def shape_constants():
    c = np.zeros((P, C_ALL), np.float32)
    c[:, C_ID:C_ID + P] = np.eye(P)
    for k in range(KV):
        c[HD * k:HD * (k + 1), C_KVMASK + k] = 1.0
    ones = c[:, C_ONES:C_ONES + 4 * HD].reshape(P, 2, 2 * HD)
    ones[:, 0, :HD] = 1.0
    ones[:, 1, HD:] = 1.0
    c[:, C_ONES:C_ONES + 4 * HD] = ones.reshape(P, -1)
    for g in range(G):
        c[g * KV:(g + 1) * KV, C_GMASK + g * P:C_GMASK + (g + 1) * P] = 1.0
        for k in range(KV):
            c[g * KV + k, C_SEL + k] = 1.0
    return c


def kernel(x, ctx_2048, mask_Bx1xSxS2_ff0, L0_xattn_w_qk, L0_xattn_w_v, L0_xattn_b_v, L0_xattn_w_t, L0_xattn_b_t,
           L1_xattn_Wq, L1_xattn_bq, L1_xattn_Wk, L1_xattn_bk, L1_xattn_Wv, L1_xattn_bv, L1_xattn_Wo, L1_xattn_bo,
           L1_xattn_gamma, L1_xattn_beta):
    import concourse.bacc as bacc
    from concourse.bass_utils import run_bass_kernel_spmd

    wq = np.asarray(L1_xattn_Wq).reshape(N, KV, G, HD).transpose(0, 2, 1, 3).reshape(N, N)
    wo = np.asarray(L1_xattn_Wo).reshape(KV, G, HD, N).transpose(1, 0, 2, 3).reshape(N, N)
    bq = np.asarray(L1_xattn_bq).reshape(KV, G, HD).transpose(0, 2, 1).reshape(P, G)
    columns = np.concatenate([bq] + [np.asarray(b).reshape(P, 1) for b in (L1_xattn_bk, L1_xattn_bv, L0_xattn_b_v)], 1)
    arrays = {
        "in_x": x, "in_ctx": ctx_2048, "in_mask": mask_Bx1xSxS2_ff0, "in_w_qk": L0_xattn_w_qk, "in_w_v": L0_xattn_w_v,
        "in_w_t": L0_xattn_w_t, "in_b_t": L0_xattn_b_t, "in_Wq": wq, "in_Wk": L1_xattn_Wk, "in_Wv": L1_xattn_Wv,
        "in_Wo": wo, "in_bo": L1_xattn_bo, "in_gamma": L1_xattn_gamma, "in_beta": L1_xattn_beta,
        "in_columns": columns, "shape_constants": shape_constants(),
    }
    arrays = {n: np.ascontiguousarray(a) for n, a in arrays.items()}
    nc = bacc.Bacc("TRN2", target_bir_lowering=False, num_devices=1)
    args = [nc.dram_tensor(n, a.shape, mybir.dt.from_np(a.dtype), kind="ExternalInput").ap() for n, a in arrays.items()]
    out = nc.dram_tensor("out_x", (B, P, N), F32, kind="ExternalOutput").ap()
    build_xattn(nc, *args, out)
    r = run_bass_kernel_spmd(nc, [arrays], core_ids=[0])
    return r.results[0]["out_x"]
```

```python
from contextlib import ExitStack

import numpy as np

import concourse.bass as bass
from concourse import mybir

F32 = mybir.dt.float32
F32R = mybir.dt.float32r
I32 = mybir.dt.int32
ALU = mybir.AluOpType
ACT = mybir.ActivationFunctionType
AX = mybir.AxisListType

P = 128
B = 32
PAIRS = B // 2
N = 512
KC = N // P
KV = 8
G = 4
HD = 16
SCALE = 0.25
COL_EPS = 1e-7
LN_EPS = 1e-6

ONE = P
A0 = P + 2
X0 = A0 + P
CW = X0 + P
BW = P + 2

C_ID = 0
C_KVMASK = C_ID + P
C_ONES = C_KVMASK + KV
C_GMASK = C_ONES + 2 * 2 * HD
C_SEL = C_GMASK + G * P
C_LN = C_SEL + KV
LN_CONSTANTS = (1.0 / N, LN_EPS, 0.25, -0.5, 1.5)
C_ALL = C_LN + len(LN_CONSTANTS)

GEN_USES = (
    [(f"q{g}", 2) for g in range(G)]
    + [("r0", 2), ("r1", 2), ("m0", 2), ("m1", 2)]
    + [("et0", 1), ("et1", 1), ("wo0", 2), ("k", 1), ("v", 1), ("vt0", 1), ("vt1", 1)]
    + [("z0", 0), ("z1", 0), ("wo1", 2)]
)
WIDE_USES = (
    [(f"tva0{k}", 1) for k in range(KC)]
    + [("tva10", 1), ("tva11", 1), ("mx000", 2), ("mx001", 2), ("en00", 1), ("tva12", 1), ("tva13", 1)]
    + [u for g in range(1, G) for u in ((f"mx0{g}0", 2), (f"mx0{g}1", 2), (f"en0{g}", 1))]
    + [("en10", 1)]
    + [u for kv in range(KV) for u in ((f"st0{kv}", 2), (f"mx1{kv // 2}{kv % 2}", 2))]
    + [(f"st1{kv}", 2) for kv in range(4)]
    + [u for n in range(1, KC) for u in ((f"en1{n}", 1), (f"st1{3 + n}", 2))]
    + [("st17", 2)]
    + [(f"b{j}{h}", 1) for j in range(2) for h in range(2)]
)
GEN_SLOTS, WIDE_SLOTS = 2, 4


def ring(uses, slots, stages, stages_before):
    now = [n for n, s in uses if s in stages]
    before = [n for n, s in uses if s in stages_before]
    assert len(now) % slots == 0 and len(before) % slots == 0
    plan = {}
    for at, name in enumerate(now):
        if at >= slots:
            plan[name] = (at % slots, now[at - slots], 0)
        elif before:
            plan[name] = (at % slots, before[len(before) - slots + at], 1)
        else:
            plan[name] = (at % slots, None, 0)
    return plan


def build_xattn(nc, x, ctx, mask, w_qk, w_v, w_t, b_t, Wq, Wk, Wv, Wo, bo, gamma, beta, columns, consts, out):
    es = ExitStack()
    with es:
        def sb(name, shape, dt=F32):
            return es.enter_context(nc.sbuf_tensor(name, shape, dt))

        def ps(name, shape):
            return es.enter_context(nc.psum_tensor(name, shape, F32))

        cst = sb("cst", [P, C_ALL])
        ident = cst[:, C_ID:C_ID + P]
        kvmask = cst[:, C_KVMASK:C_KVMASK + KV]
        ones_eo = cst[:, C_ONES:C_ONES + 4 * HD].rearrange("p (o c) -> p o c", o=2)
        gmask = cst[0:64, C_GMASK:C_GMASK + G * P]
        sel_f = cst[0:64, C_SEL:C_SEL + KV]
        per_n, ln_eps, quarter, minus_half, three_halves = (
            cst[:, c:c + 1].broadcast_to([P, 2]) for c in range(C_LN, C_ALL))
        sel = sb("sel", [2 * G * KV, KV], F32R)
        ident4 = sb("ident4", [P, G, P], F32R)
        cols = sb("cols", [P, G + 3])
        bq_raw, bk_s, bv_s, b0_s = cols[:, 0:G], cols[:, G:G + 1], cols[:, G + 1:G + 2], cols[:, G + 2:G + 3]
        gram_h = sb("gram_h", [P, P], F32R)
        gram_l = sb("gram_l", [P, P], F32R)
        cw_h = sb("cw_h", [P, CW], F32R)
        cw_l = sb("cw_l", [P, CW], F32R)
        cb_s = sb("cb_s", [P, CW])
        att = sb("att", [P, 2, KC, N])
        setup = att[:].rearrange("p a b n -> p (a b n)")
        stage_kv = setup[:, 0:2 * N].rearrange("p (w k c) -> p w k c", w=2, k=KC)
        cw_s = setup[:, 4 * N:4 * N + CW]
        wqk_s, wv_s, wt_s, wtT_s = (setup[:, 5 * N + n * P:5 * N + (n + 1) * P] for n in range(4))
        late = sb("late", [P, 4, 2, N])
        stage_w = late[:, 0:2].rearrange("p a b n -> p (a b) n")
        wtmp = late[:, 2:4].rearrange("p a b n -> p (a b) n")
        wq_h = sb("wq_h", [P, KC, G, P], F32R)
        wq_l = sb("wq_l", [P, KC, G, P], F32R)
        wkv_h = sb("wkv_h", [P, 2, KC, P], F32R)
        wkv_l = sb("wkv_l", [P, 2, KC, P], F32R)
        wo_h = sb("wo_h", [P, G, N], F32R)
        wo_l = sb("wo_l", [P, G, N], F32R)
        bq_s = sb("bq_s", [P, G])
        bo_b = sb("bo_b", [P, N])
        gamma_b = sb("gamma_b", [P, N])
        beta_b = sb("beta_b", [P, N])
        flag_col = sb("flag_col", [P, 1])
        flag_i = sb("flag_i", [1, 1], I32)

        xs = sb("xs", [P, 2, N])
        ys = sb("ys", [P, 2, N])
        mk = sb("mk", [P, 2, P])
        xh = sb("xh", [P, 2, N], F32R)
        xl = sb("xl", [P, 2, N], F32R)
        yh = sb("yh", [P, 2, N], F32R)
        yl = sb("yl", [P, 2, N], F32R)
        zh = sb("zh", [P, 2, N], F32R)
        zl = sb("zl", [P, 2, N], F32R)
        ta = sb("ta", [P, 2, KC, CW])
        negmax = sb("negmax", [P, 2, KC])
        rowsum = sb("rowsum", [P, 2, KC])
        rowinv = sb("rowinv", [P, 2, KC])
        colneg = sb("colneg", [P, 2, KC])
        colinv = sb("colinv", [P, 2, KC])
        x2 = sb("x2", [P, KC, 2, P])
        x2h = sb("x2h", [P, KC, 2, P], F32R)
        x2l = sb("x2l", [P, KC, 2, P], F32R)
        eth = sb("eth", [P, KC, 2, P], F32R)
        etl = sb("etl", [P, KC, 2, P], F32R)
        kh = sb("kh", [P, 2, P], F32R)
        kl = sb("kl", [P, 2, P], F32R)
        kbh = sb("kbh", [P, 2, KV, P], F32R)
        kbl = sb("kbl", [P, 2, KV, P], F32R)
        vts = sb("vts", [P, 2, P])
        v2 = sb("v2", [P, 2, KV, 2 * HD])
        qh = sb("qh", [P, 2, G, P], F32R)
        ql = sb("ql", [P, 2, G, P], F32R)
        maxima = sb("maxima", [P, 2, G * KV])
        mrow = sb("mrow", [P, 2, 2, G * KV], F32R)
        mrep = sb("mrep", [2 * G * KV, G * P], F32R)
        prob = sb("prob", [P, KV, G * P])
        stage_o = prob[:, 0:G]
        at, xr, res, outb = (late[:, n] for n in range(4))
        ath = sb("ath", [P, G, P], F32R)
        atl = sb("atl", [P, G, P], F32R)
        bns = sb("bns", [P, 2, 6])
        mv = sb("mv", [P, 2, 2])
        nv = sb("nv", [P, 8, 2])
        yi = sb("yi", [P, 2], I32)

        wide = ps("wide", [P, WIDE_SLOTS, N])
        gen = ps("gen", [P, GEN_SLOTS, N])
        den = ps("den", [P, N])
        outt = ps("outt", [P, N])

        SEMS = dict(
            xh_done=2, x_split=2, yh_done=2, y_split=2, kb_done=4, xrb_done=2, gam_done=2, out_ready=2, ln_var=6, ln_step=13,
            z_ps=2, tva_ps=8, et_ps=2, k_ps=1, v_ps=1, vt_ps=2, en_ps=8, b_ps=4,
            q_ps=4, r_ps=2, mx_ps=16, m_ps=2, st_ps=16, den_ps=2, o_ps=2, wo_ps=2,
            zh_done=2, exp_done=8, tv_done=8, eth_done=2, kh_done=1, vts_done=1, v2_done=4, x2h_done=2,
            qh_done=4, xr_done=2, prob_done=16, ath_done=2, nrm_done=2,
            zl_done=2, ta_done=8, negmax_done=8, rowinv_done=2, colneg_done=2, colinv_done=2, pre_done=8,
            x2_done=2, x2l_done=2, etl_done=2, kl_done=1, ql_done=4, max_done=16, mrow_done=4, mrep_done=2, dinv_done=2,
            at_done=2, atl_done=2, res_done=2, bns_done=2, ln_sums=1, ln_guess=1,
        )
        sem = {k: es.enter_context(nc.semaphore(k)) for k in SEMS}
        x_in = es.enter_context(nc.semaphore("x_in"))
        y_in = es.enter_context(nc.semaphore("y_in"))
        mask_in = es.enter_context(nc.semaphore("mask_in"))
        out_sem = [es.enter_context(nc.semaphore(f"out_done{j}")) for j in range(2)]
        w0_in = es.enter_context(nc.semaphore("w0_in"))
        w1_in = es.enter_context(nc.semaphore("w1_in"))
        allmask_in = es.enter_context(nc.semaphore("allmask_in"))
        setup_pe = es.enter_context(nc.semaphore("setup_pe"))
        setup_dve = es.enter_context(nc.semaphore("setup_dve"))
        cw_ready = es.enter_context(nc.semaphore("cw_ready"))
        weights_ready = es.enter_context(nc.semaphore("weights_ready"))
        flag_ps = es.enter_context(nc.semaphore("flag_ps"))
        flag_ready = es.enter_context(nc.semaphore("flag_ready"))
        zeros_ready = es.enter_context(nc.semaphore("zeros_ready"))

        def wait(eng, name, pair, n):
            value = pair * SEMS[name] + (n + 1)
            if isinstance(value, int) and value <= 0:
                return
            eng.wait_ge(sem[name], value)

        RELEASE = {}
        for j in range(2):
            RELEASE[f"z{j}"] = ("zl_done", j, 0)
            RELEASE[f"et{j}"] = ("etl_done", j, 1)
            RELEASE[f"vt{j}"] = ("v2_done", 2 * j + 1, 1)
            RELEASE[f"r{j}"] = ("xr_done", j, 2)
            RELEASE[f"m{j}"] = ("mrep_done", j, 2)
            RELEASE[f"wo{j}"] = ("res_done", j, 2)
            for k in range(4):
                RELEASE[f"tva{j}{k}"] = ("ta_done", 4 * j + k, 1)
                RELEASE[f"en{j}{k}"] = ("exp_done", 4 * j + k, 1)
            for h in range(2):
                RELEASE[f"b{j}{h}"] = ("pre_done", 4 * j + 2 * h + 1, 1)
            for kv in range(KV):
                RELEASE[f"mx{j}{kv // 2}{kv % 2}"] = ("max_done", 8 * j + kv, 2)
                RELEASE[f"st{j}{kv}"] = ("prob_done", 8 * j + kv, 2)
        for g in range(G):
            RELEASE[f"q{g}"] = ("ql_done", g, 2)
        RELEASE["k"] = ("kl_done", 0, 1)
        RELEASE["v"] = ("vts_done", 0, 1)

        def plans(stages, before):
            return {**ring(GEN_USES, GEN_SLOTS, stages, before), **ring(WIDE_USES, WIDE_SLOTS, stages, before)}

        def slot(plan, name):
            return plan[name][0]

        def wait_slot(eng, plan, name, i):
            _, prev, back = plan[name]
            if prev is not None:
                signal, n, stage = RELEASE[prev]
                wait(eng, signal, i - back + 1 - stage, n)

        START = plans((0,), ())
        FIRST = plans((0, 1), (0,))
        SECOND = plans((0, 1, 2), (0, 1))
        FULL = plans((0, 1, 2), (0, 1, 2))
        NEXT_TO_LAST = plans((1, 2), (0, 1, 2))
        LAST = plans((2,), (1, 2))

        block = es.enter_context(nc.Block())

        @block.sync
        def _(sp):
            def load_x(pair):
                sp.dma_start(xs[:], x[bass.ts(pair, 2)].rearrange("b c n -> c b n")).then_inc(x_in, 16)

            def load_y(pair):
                sp.dma_start(ys[:], ctx[bass.ts(pair, 2)].rearrange("b c n -> c b n")).then_inc(y_in, 16)

            def load_mask(pair):
                sp.dma_start(mk[:], mask[bass.ts(pair, 2)].rearrange("b o l s -> l (b o) s")).then_inc(mask_in, 16)

            def store(pair, j):
                sp.dma_start(out[bass.ds(pair * 2 + j, 1)].rearrange("b l h -> l b h"),
                             outb[:, j:j + 1, :]).then_inc(out_sem[j], 16)

            def iteration(i, load_next, s1, s3):
                if load_next:
                    wait(sp, "x_split", i, 1)
                    load_x(i + 1)
                if s1:
                    if not isinstance(i, int) or i > 0:
                        sp.wait_ge(mask_in, i * 16)
                    wait(sp, "st_ps", i - 1, 15)
                    load_mask(i)
                if load_next:
                    wait(sp, "y_split", i, 1)
                    wait(sp, "et_ps", i, 1)
                    load_y(i + 1)
                if s3:
                    for j in range(2):
                        wait(sp, "out_ready", i - 2, j)
                        store(i - 2, j)

            load_x(0)
            load_y(0)
            for dst, src in ((cst[:], consts), (wqk_s, w_qk), (wv_s, w_v), (wt_s, w_t),
                             (cols[:], columns),
                             (cb_s[:, A0:A0 + P], b_t.partition_broadcast(P))):
                sp.dma_start(dst, src).then_inc(w0_in, 16)
            sp.dma_start(stage_kv[:, 0], Wk.rearrange("(k p) n -> p k n", p=P)).then_inc(w0_in, 16)
            sp.dma_start(stage_kv[:, 1], Wv.rearrange("(k p) n -> p k n", p=P)).then_inc(w0_in, 16)
            sp.dma_start(stage_w, Wq.rearrange("(k p) n -> p k n", p=P)).then_inc(w1_in, 16)
            sp.dma_start(bo_b[:], bo.partition_broadcast(P)).then_inc(w1_in, 16)
            sp.dma_start(gamma_b[:], gamma.partition_broadcast(P)).then_inc(w1_in, 16)
            sp.dma_start(beta_b[:], beta.partition_broadcast(P)).then_inc(w1_in, 16)
            sp.dma_start(prob[:].rearrange("p k n -> p (k n)"),
                         mask.rearrange("b o l s -> (b o l s)").rearrange("(p f) -> p f", p=P)
                         ).then_inc(allmask_in, 16)
            iteration(0, True, True, False)
            sp.wait_ge(setup_dve, 5)
            sp.dma_start(stage_o, Wo.rearrange("(g p) n -> p g n", g=G)).then_inc(w1_in, 16)

            iteration(1, True, True, False)
            iteration(2, True, True, True)
            with sp.Fori(3, PAIRS - 1) as i:
                iteration(i, True, True, True)
            iteration(PAIRS - 1, False, True, True)
            iteration(PAIRS, False, False, True)
            iteration(PAIRS + 1, False, False, True)
            for j in range(2):
                sp.wait_ge(out_sem[j], 16 * PAIRS)

        @block.gpsimd
        def _(pool):
            one_col = ones_eo[:, 0, 0:1].broadcast_to([P, N])
            nc.gpsimd.memset(v2[:], 0.0).then_inc(zeros_ready, 1)

            def split_x(i, j):
                if j == 0:
                    pool.wait_ge(x_in, i * 16 + 16)
                wait(pool, "tva_ps", i - 1, 4 * j + 3)
                nc.gpsimd.tensor_tensor(xh[:, j], xs[:, j], one_col, ALU.mult).then_inc(sem["xh_done"], 1)
                wait(pool, "xh_done", i, j)
                nc.gpsimd.tensor_tensor(xl[:, j], xs[:, j], xh[:, j].bitcast(F32), ALU.subtract
                                        ).then_inc(sem["x_split"], 1)

            def split_y(i, j):
                if j == 0:
                    pool.wait_ge(y_in, i * 16 + 16)
                wait(pool, "en_ps", i - 1, 4 * j + 3)
                nc.gpsimd.tensor_tensor(yh[:, j], ys[:, j], one_col, ALU.mult).then_inc(sem["yh_done"], 1)
                wait(pool, "yh_done", i, j)
                nc.gpsimd.tensor_tensor(yl[:, j], ys[:, j], yh[:, j].bitcast(F32), ALU.subtract
                                        ).then_inc(sem["y_split"], 1)

            def spread_k(i, j):
                if j == 0:
                    wait(pool, "kl_done", i, 0)
                    wait(pool, "st_ps", i - 1, 15)
                shape = [P, KV, P]
                for src, dst in ((kh, kbh), (kl, kbl)):
                    nc.gpsimd.tensor_tensor(dst[:, j], src[:, j].bitcast(F32).unsqueeze(1).broadcast_to(shape),
                                            kvmask.unsqueeze(2).broadcast_to(shape), ALU.mult
                                            ).then_inc(sem["kb_done"], 1)

            def residual_bias(q, j):
                wait(pool, "xr_done", q, j)
                nc.gpsimd.tensor_tensor(xr[:, j], xr[:, j], bo_b[:], ALU.add).then_inc(sem["xrb_done"], 1)

            def scale_shift(q, j):
                wait(pool, "nrm_done", q, j)
                store_before = q * 16
                if not isinstance(store_before, int) or store_before > 0:
                    pool.wait_ge(out_sem[j], store_before)
                nc.gpsimd.tensor_tensor(outb[:, j], res[:, j], gamma_b[:], ALU.mult).then_inc(sem["gam_done"], 1)
                wait(pool, "gam_done", q, j)
                nc.gpsimd.tensor_tensor(outb[:, j], outb[:, j], beta_b[:], ALU.add).then_inc(sem["out_ready"], 1)

            def variance(q):
                step = [0]

                def link(ins):
                    ins.then_inc(sem["ln_var"], 1)
                    wait(pool, "ln_var", q, step[0])
                    step[0] += 1

                op = nc.gpsimd.tensor_tensor
                v, t, dev = nv[:, 0], nv[:, 4], nv[:, 5]
                wait(pool, "bns_done", q, 1)
                wait(pool, "nrm_done", q - 1, 1)
                op(mv[:], bns[:, :, 1:3], bns[:, :, 4:6], ALU.add)
                link(op(dev, bns[:, :, 1], bns[:, :, 4], ALU.subtract))
                op(t, mv[:, :, 1], per_n, ALU.mult)
                link(op(dev, dev, dev, ALU.mult))
                op(t, t, ln_eps, ALU.add)
                link(op(dev, dev, quarter, ALU.mult))
                link(op(v, t, dev, ALU.add))
                link(op(nv[:, 1], v, minus_half, ALU.mult))
                link(op(nv[:, 7], mv[:, :, 0], minus_half, ALU.mult))

            def newton_root(q):
                step = [0]

                def link(ins):
                    ins.then_inc(sem["ln_step"], 1)
                    wait(pool, "ln_step", q, step[0])
                    step[0] += 1

                op = nc.gpsimd.tensor_tensor
                half, t, dev, shift = nv[:, 1], nv[:, 4], nv[:, 5], nv[:, 7]
                wait(pool, "ln_guess", q, 0)
                for old, new in ((yi[:].bitcast(F32), nv[:, 2]), (nv[:, 2], nv[:, 3]), (nv[:, 3], nv[:, 6])):
                    link(op(t, old, old, ALU.mult))
                    link(op(dev, t, half, ALU.mult))
                    link(op(t, dev, three_halves, ALU.add))
                    link(op(new, t, old, ALU.mult))
                link(op(shift, shift, nv[:, 6], ALU.mult))

            def iteration(i, s1, s2, s3, split_next):
                if split_next:
                    split_x(i + 1, 0)
                    split_x(i + 1, 1)
                if s2:
                    residual_bias(i - 1, 0)
                    residual_bias(i - 1, 1)
                if s3:
                    variance(i - 2)
                    newton_root(i - 2)
                if s3:
                    scale_shift(i - 2, 0)
                    scale_shift(i - 2, 1)
                for j in range(2):
                    if s1:
                        spread_k(i, j)
                    if split_next:
                        split_y(i + 1, j)

            pool.wait_ge(w0_in, 16 * 8)
            for j in range(2):
                split_x(0, j)
            for j in range(2):
                split_y(0, j)
            iteration(0, True, False, False, True)
            pool.wait_ge(w1_in, 16 * 5)
            iteration(1, True, True, False, True)
            iteration(2, True, True, True, True)
            with pool.Fori(3, PAIRS - 1) as i:
                iteration(i, True, True, True, True)
            iteration(PAIRS - 1, True, True, True, False)
            iteration(PAIRS, False, True, True, False)
            iteration(PAIRS + 1, False, False, True, False)

        @block.tensor
        def _(pe):
            mm = nc.tensor.matmul

            pe.wait_ge(w0_in, 16 * 8)
            mm(gen[:, 0, 0:P], wqk_s, wqk_s, start=True, stop=True)
            nc.tensor.transpose(den[:, 0:P], wt_s, ident).then_inc(setup_pe, 1)
            pe.wait_ge(setup_dve, 2)
            mm(gen[:, 1, 0:P], wv_s, wtT_s, start=True, stop=True)
            mm(outt[:, 0:P], b0_s.broadcast_to([P, P]), wtT_s, start=True, stop=True).then_inc(setup_pe, 1)
            pe.wait_ge(cw_ready, 1)

            def z_project(i, plan, j):
                wait(pe, "x_split", i + 1, j)
                wait_slot(pe, plan, f"z{j}", i)
                o = gen[:, slot(plan, f"z{j}")]
                mm(o, gram_h[:], xh[:, j], start=True, stop=False)
                mm(o, gram_h[:], xl[:, j], start=False, stop=False)
                mm(o, gram_l[:], xh[:, j], start=False, stop=True).then_inc(sem["z_ps"], 1)

            def tva_project(i, plan, j, k):
                name = f"tva{j}{k}"
                wait_slot(pe, plan, name, i)
                o = wide[:, slot(plan, name)]
                a, b = xh[:, j, bass.ts(k, P)], xl[:, j, bass.ts(k, P)]
                mm(o[:, 0:CW], a, cw_h[:], start=True, stop=False)
                mm(o[:, 0:CW], b, cw_h[:], start=False, stop=False)
                mm(o[:, 0:X0], a, cw_l[:, 0:X0], start=False, stop=True).then_inc(sem["tva_ps"], 1)

            def energy(i, plan, j, n):
                name = f"en{j}{n}"
                if n == 0:
                    wait(pe, "zl_done", i, j)
                    wait(pe, "y_split", i, j)
                wait_slot(pe, plan, name, i)
                o = wide[:, slot(plan, name)]
                a, b = yh[:, j, bass.ts(n, P)], yl[:, j, bass.ts(n, P)]
                mm(o, a, zh[:, j], start=True, stop=False)
                mm(o, a, zl[:, j], start=False, stop=False)
                mm(o, b, zh[:, j], start=False, stop=True).then_inc(sem["en_ps"], 1)

            def attend(i, plan, j, h):
                name = f"b{j}{h}"
                if h == 0:
                    wait(pe, "tv_done", i, 4 * j + 3)
                wait_slot(pe, plan, name, i)
                for half in range(2):
                    m = 2 * h + half
                    o = wide[:, slot(plan, name), half * 256:half * 256 + BW]
                    for n in range(KC):
                        last = mm(o, att[:, j, n, bass.ts(m, P)], ta[:, j, n, 0:BW], start=n == 0, stop=n == KC - 1)
                last.then_inc(sem["b_ps"], 1)

            def ctx_transpose(i, plan, j):
                name = f"et{j}"
                if j == 0:
                    pe.wait_ge(y_in, i * 16 + 16)
                wait_slot(pe, plan, name, i)
                for k in range(KC):
                    last = nc.tensor.transpose(gen[:, slot(plan, name), bass.ts(k, P)], ys[:, j, bass.ts(k, P)], ident)
                last.then_inc(sem["et_ps"], 1)

            def kv_project(i, plan, name, n, done):
                wait(pe, "etl_done", i, 1)
                wait_slot(pe, plan, name, i)
                o = gen[:, slot(plan, name), 0:2 * P]
                for k in range(KC):
                    mm(o, wkv_h[:, n, k], eth[:, k], start=k == 0, stop=False)
                    mm(o, wkv_h[:, n, k], etl[:, k], start=False, stop=False)
                    last = mm(o, wkv_l[:, n, k], eth[:, k], start=False, stop=k == KC - 1)
                last.then_inc(sem[done], 1)

            def v_transpose(i, plan, j):
                name = f"vt{j}"
                wait(pe, "vts_done", i, 0)
                wait_slot(pe, plan, name, i)
                nc.tensor.transpose(gen[:, slot(plan, name), 0:P], vts[:, j], ident).then_inc(sem["vt_ps"], 1)

            def q_project(q, plan, i, g):
                name = f"q{g}"
                if g == 0:
                    wait(pe, "x2l_done", q, 1)
                wait_slot(pe, plan, name, i)
                o = gen[:, slot(plan, name), 0:2 * P]
                for k in range(KC):
                    mm(o, wq_h[:, k, g], x2h[:, k], start=k == 0, stop=False)
                    mm(o, wq_h[:, k, g], x2l[:, k], start=False, stop=False)
                    last = mm(o, wq_l[:, k, g], x2h[:, k], start=False, stop=k == KC - 1)
                last.then_inc(sem["q_ps"], 1)

            def residual_transpose(q, plan, i, j):
                name = f"r{j}"
                wait(pe, "x2_done", q, j)
                wait_slot(pe, plan, name, i)
                for k in range(KC):
                    last = nc.tensor.transpose(gen[:, slot(plan, name), bass.ts(k, P)], x2[:, k, j], ident)
                last.then_inc(sem["r_ps"], 1)

            def max_scores(q, plan, i, j, g, half, masked):
                name = f"mx{j}{g}{half}"
                if half == 0:
                    wait(pe, "ql_done", q, g)
                if g == 0 and half == 0:
                    wait(pe, "kb_done", q, 2 * j + 1)
                wait_slot(pe, plan, name, i)
                o = wide[:, slot(plan, name)]
                last = mm(o, qh[:, j, g], kbh[:, j, 4 * half:4 * half + 4], start=True, stop=not masked)
                if masked:
                    last = mm(o, ident, mk[:, j].unsqueeze(1).broadcast_to([P, 4, P]), start=False, stop=True)
                last.then_inc(sem["mx_ps"], 1)

            def max_spread(q, plan, i, j):
                name = f"m{j}"
                wait(pe, "mrow_done", q, 2 * j + 1)
                wait_slot(pe, plan, name, i)
                mm(gen[0:64, slot(plan, name)], mrow[:, j], ident4[:], start=True, stop=True).then_inc(sem["m_ps"], 1)

            def scores(q, plan, i, j, kv, masked):
                name = f"st{j}{kv}"
                if kv == 0:
                    wait(pe, "mrep_done", q, j)
                wait_slot(pe, plan, name, i)
                o = wide[:, slot(plan, name)]
                mm(o, kbh[:, j, kv], qh[:, j], start=True, stop=False)
                mm(o, kbh[:, j, kv], ql[:, j], start=False, stop=False)
                mm(o, kbl[:, j, kv], qh[:, j], start=False, stop=False)
                last = mm(o, sel[:, kv:kv + 1].broadcast_to([2 * G * KV, P]), mrep[:], start=False, stop=not masked)
                if masked:
                    last = mm(o, mk[:, j], ident.unsqueeze(1).broadcast_to([P, G, P]), start=False, stop=True)
                last.then_inc(sem["st_ps"], 1)

            def weigh(q, j, dst, operand, done):
                wait(pe, "prob_done", q, 8 * j + 7)
                wait(pe, "at_done", q, j - 1)
                for odd in range(2):
                    for p in range(KV // 2):
                        last = mm(dst[32 * p:32 * p + 32, :], operand(2 * p + odd, odd), prob[:, 2 * p + odd],
                                  start=odd == 0, stop=odd == 1, tile_position=(0, 32 * p))
                last.then_inc(sem[done], 1)

            def denominators(q, j):
                weigh(q, j, den, lambda kv, odd: ones_eo[:, odd], "den_ps")

            def values(q, j):
                if j == 0:
                    wait(pe, "v2_done", q, 3)
                weigh(q, j, outt, lambda kv, odd: v2[:, j, kv], "o_ps")

            def out_project(q, plan, i, j):
                name = f"wo{j}"
                wait(pe, "atl_done", q, j)
                wait_slot(pe, plan, name, i)
                o = gen[:, slot(plan, name)]
                for g in range(G):
                    mm(o, ath[:, g], wo_h[:, g], start=g == 0, stop=False)
                    mm(o, ath[:, g], wo_l[:, g], start=False, stop=False)
                    last = mm(o, atl[:, g], wo_h[:, g], start=False, stop=g == G - 1)
                last.then_inc(sem["wo_ps"], 1)

            def iteration(i, plan, s0, s1, s2, masked):
                q = i - 1
                if s1:
                    for k in range(KC):
                        tva_project(i, plan, 0, k)
                if s2:
                    q_project(q, plan, i, 0)
                if s1:
                    tva_project(i, plan, 1, 0)
                    tva_project(i, plan, 1, 1)
                for g in range(G):
                    if s2:
                        if g + 1 < G:
                            q_project(q, plan, i, g + 1)
                        max_scores(q, plan, i, 0, g, 0, masked)
                        max_scores(q, plan, i, 0, g, 1, masked)
                    if s1:
                        energy(i, plan, 0, g)
                        if g == 0:
                            tva_project(i, plan, 1, 2)
                            tva_project(i, plan, 1, 3)
                if s2:
                    residual_transpose(q, plan, i, 0)
                    residual_transpose(q, plan, i, 1)
                    max_spread(q, plan, i, 0)
                if s1:
                    energy(i, plan, 1, 0)
                if s2:
                    for kv in range(KV):
                        scores(q, plan, i, 0, kv, masked)
                        max_scores(q, plan, i, 1, kv // 2, kv % 2, masked)
                    denominators(q, 0)
                    max_spread(q, plan, i, 1)
                    values(q, 0)
                    for kv in range(4):
                        scores(q, plan, i, 1, kv, masked)
                for n in range(1, KC):
                    if s1:
                        energy(i, plan, 1, n)
                    if s2:
                        scores(q, plan, i, 1, 3 + n, masked)
                if s2:
                    scores(q, plan, i, 1, 7, masked)
                if s1:
                    ctx_transpose(i, plan, 0)
                    ctx_transpose(i, plan, 1)
                if s2:
                    out_project(q, plan, i, 0)
                if s1:
                    kv_project(i, plan, "k", 0, "k_ps")
                    kv_project(i, plan, "v", 1, "v_ps")
                if s2:
                    denominators(q, 1)
                if s1:
                    v_transpose(i, plan, 0)
                    v_transpose(i, plan, 1)
                if s2:
                    values(q, 1)
                if s0:
                    z_project(i, plan, 0)
                    z_project(i, plan, 1)
                if s1:
                    for j in range(2):
                        attend(i, plan, j, 0)
                        attend(i, plan, j, 1)
                if s2:
                    out_project(q, plan, i, 1)

            iteration(-1, START, True, False, False, False)
            iteration(0, FIRST, True, True, False, False)
            pe.wait_ge(setup_dve, 5)
            mm(den[0:1, 0:1], flag_col[:], ones_eo[:, 0, 0:1], start=True, stop=True).then_inc(flag_ps, 1)
            pe.wait_ge(weights_ready, 1)
            pe.wait_ge(flag_ready, 1)
            any_mask = pe.value_load(flag_i[0:1, 0:1], min_val=0, max_val=1)

            def rest(masked):
                if masked:
                    pe.wait_ge(mask_in, 16)
                iteration(1, SECOND, True, True, True, masked)
                with pe.Fori(2, PAIRS - 1) as i:
                    if masked:
                        pe.wait_ge(mask_in, i * 16)
                    iteration(i, FULL, True, True, True, masked)
                if masked:
                    pe.wait_ge(mask_in, (PAIRS - 1) * 16)
                iteration(PAIRS - 1, NEXT_TO_LAST, False, True, True, masked)
                if masked:
                    pe.wait_ge(mask_in, PAIRS * 16)
                iteration(PAIRS, LAST, False, False, True, masked)

            with pe.If(any_mask > 0):
                rest(True)
            with pe.Else():
                rest(False)

        @block.scalar
        def _(act):
            ident_f, copy_f, exp_f = ACT.Identity, ACT.Copy, ACT.Exp

            def z_high(i, plan, j):
                wait(act, "z_ps", i + 1, j)
                wait(act, "en_ps", i, 4 * j + 3)
                nc.scalar.activation(zh[:, j], gen[:, slot(plan, f"z{j}")], copy_f).then_inc(sem["zh_done"], 1)

            def exp_energy(i, plan, j, n):
                wait(act, "negmax_done", i, 4 * j + n)
                wait(act, "b_ps", i - 1, 2 * j + 1)
                nc.scalar.activation(att[:, j, n], wide[:, slot(plan, f"en{j}{n}")], exp_f,
                                     bias=negmax[:, j, n:n + 1], accum_out=rowsum[:, j, n:n + 1]
                                     ).then_inc(sem["exp_done"], 1)

            def scale_values(i, j):
                wait(act, "rowinv_done", i, j)
                for n in range(KC):
                    nc.scalar.activation(ta[:, j, n, 0:BW], ta[:, j, n, 0:BW], copy_f,
                                         scale=rowinv[:, j, n:n + 1]).then_inc(sem["tv_done"], 1)

            def ctx_high(i, plan, j):
                wait(act, "et_ps", i, j)
                wait(act, "v_ps", i - 1, 0)
                nc.scalar.activation(eth[:, :, j], gen[:, slot(plan, f"et{j}")].rearrange("p (k s) -> p k s", k=KC),
                                     copy_f).then_inc(sem["eth_done"], 1)

            def k_high(i, plan):
                wait(act, "k_ps", i, 0)
                wait(act, "kb_done", i - 1, 3)
                nc.scalar.activation(kh[:], gen[:, slot(plan, "k"), 0:2 * P].rearrange("p (j s) -> p j s", j=2),
                                     ident_f, bias=bk_s).then_inc(sem["kh_done"], 1)

            def v_biased(i, plan):
                wait(act, "v_ps", i, 0)
                wait(act, "vt_ps", i - 1, 1)
                nc.scalar.activation(vts[:], gen[:, slot(plan, "v"), 0:2 * P].rearrange("p (j s) -> p j s", j=2),
                                     ident_f, bias=bv_s).then_inc(sem["vts_done"], 1)

            def v_place(i, plan, j):
                wait(act, "vt_ps", i, j)
                wait(act, "o_ps", i - 1, 1)
                src = gen[:, slot(plan, f"vt{j}"), 0:P].rearrange("p (k o d) -> p k o d", o=2, d=HD)
                dst = v2[:, j].rearrange("p (k o) c -> p k o c", o=2)
                for odd in range(2):
                    nc.scalar.activation(dst[:, :, odd, HD * odd:HD * odd + HD], src[:, :, odd], copy_f
                                         ).then_inc(sem["v2_done"], 1)

            def x2_high(i, j):
                wait(act, "x2_done", i, j)
                wait(act, "q_ps", i - 1, 3)
                nc.scalar.activation(x2h[:, :, j], x2[:, :, j], copy_f).then_inc(sem["x2h_done"], 1)

            def q_high(q, plan, g):
                wait(act, "q_ps", q, g)
                wait(act, "st_ps", q - 1, 15)
                nc.scalar.activation(qh[:, :, g], gen[:, slot(plan, f"q{g}"), 0:2 * P].rearrange("p (j l) -> p j l", j=2),
                                     ident_f, bias=bq_s[:, g:g + 1]).then_inc(sem["qh_done"], 1)

            def residual(q, plan, j):
                wait(act, "r_ps", q, j)
                wait(act, "res_done", q - 1, j)
                nc.scalar.activation(xr[:, j], gen[:, slot(plan, f"r{j}")], copy_f).then_inc(sem["xr_done"], 1)

            def exp_scores(q, plan, j, kv):
                wait(act, "st_ps", q, 8 * j + kv)
                if kv == 0:
                    wait(act, "o_ps", q, j - 1)
                nc.scalar.activation(prob[:, kv], wide[:, slot(plan, f"st{j}{kv}")], exp_f
                                     ).then_inc(sem["prob_done"], 1)

            def at_high(q, j):
                wait(act, "at_done", q, j)
                wait(act, "wo_ps", q, j - 1)
                nc.scalar.activation(ath[:], at[:, j].rearrange("p (g l) -> p g l", g=G), copy_f
                                     ).then_inc(sem["ath_done"], 1)

            def normalise(q, j):
                wait(act, "ln_step", q, 12)
                nc.scalar.activation(res[:, j], res[:, j], ident_f, bias=nv[:, 7, j:j + 1], scale=nv[:, 6, j:j + 1]
                                     ).then_inc(sem["nrm_done"], 1)

            def iteration(i, plan, s0, s1, s2, s3):
                q = i - 1
                if s2:
                    q_high(q, plan, 0)
                    q_high(q, plan, 1)
                for n in range(KC):
                    if s2:
                        if n + 2 < G:
                            q_high(q, plan, n + 2)
                    if s1:
                        exp_energy(i, plan, 0, n)
                if s2:
                    residual(q, plan, 0)
                    residual(q, plan, 1)
                if s1:
                    exp_energy(i, plan, 1, 0)
                if s2:
                    for kv in range(4):
                        exp_scores(q, plan, 0, kv)
                if s1:
                    scale_values(i, 0)
                if s2:
                    for kv in range(4, KV):
                        exp_scores(q, plan, 0, kv)
                    for kv in range(4):
                        exp_scores(q, plan, 1, kv)
                    at_high(q, 0)
                if s3:
                    normalise(i - 2, 0)
                    normalise(i - 2, 1)
                for n in range(1, KC):
                    if s1:
                        exp_energy(i, plan, 1, n)
                    if s2:
                        exp_scores(q, plan, 1, 3 + n)
                if s2:
                    exp_scores(q, plan, 1, 7)
                if s1:
                    ctx_high(i, plan, 0)
                    ctx_high(i, plan, 1)
                    scale_values(i, 1)
                if s1:
                    k_high(i, plan)
                    v_biased(i, plan)
                    v_place(i, plan, 0)
                    v_place(i, plan, 1)
                if s2:
                    at_high(q, 1)
                if s0:
                    z_high(i, plan, 0)
                    z_high(i, plan, 1)
                if s1:
                    x2_high(i, 0)
                    x2_high(i, 1)

            act.wait_ge(w0_in, 16 * 8)
            act.wait_ge(zeros_ready, 1)
            iteration(-1, START, True, False, False, False)
            iteration(0, FIRST, True, True, False, False)
            act.wait_ge(weights_ready, 1)
            iteration(1, SECOND, True, True, True, False)
            iteration(2, FULL, True, True, True, True)
            with act.Fori(3, PAIRS - 1) as i:
                iteration(i, FULL, True, True, True, True)
            iteration(PAIRS - 1, NEXT_TO_LAST, False, True, True, True)
            iteration(PAIRS, LAST, False, False, True, True)
            iteration(PAIRS + 1, None, False, False, False, True)

        @block.vector
        def _(dve):
            tt, stt, cp = nc.vector.tensor_tensor, nc.vector.scalar_tensor_tensor, nc.vector.tensor_copy

            dve.wait_ge(w0_in, 16 * 8)
            nc.vector.memset(cw_s[:, ONE:A0], 0.0)
            nc.vector.memset(cb_s[:, ONE:ONE + 1], 1.0)
            nc.vector.memset(cb_s[:, ONE + 1:ONE + 2], 0.0)
            nc.vector.memset(cb_s[:, X0:CW], 0.0)
            cp(cw_s[:, X0:CW], ident)
            cp(sel[:], sel_f)
            cp(ident4[:], ident.unsqueeze(1).broadcast_to([P, G, P]))
            dve.wait_ge(setup_pe, 1)
            cp(gram_h[:], gen[:, 0, 0:P]).then_inc(setup_dve, 1)
            cp(wtT_s, den[:, 0:P]).then_inc(setup_dve, 1)
            dve.wait_ge(setup_dve, 1)
            tt(gram_l[:], gen[:, 0, 0:P], gram_h[:].bitcast(F32), ALU.subtract)
            cp(cw_s[:, A0:X0], den[:, 0:P])
            dve.wait_ge(setup_pe, 2)
            cp(cb_s[:, 0:P], outt[:, 0:P])
            cp(cw_s[:, 0:P], gen[:, 1, 0:P]).then_inc(setup_dve, 1)
            dve.wait_ge(setup_dve, 3)
            cp(cw_h[:], cw_s)
            cp(wkv_h[:], stage_kv[:]).then_inc(setup_dve, 1)
            dve.wait_ge(setup_dve, 4)
            tt(wkv_l[:], stage_kv, wkv_h[:].bitcast(F32), ALU.subtract)
            tt(cw_l[:], cw_s, cw_h[:].bitcast(F32), ALU.subtract).then_inc(cw_ready, 1)

            def setup_mask_flag():
                dve.wait_ge(allmask_in, 16)
                masks = prob[:].rearrange("p k n -> p (k n)")
                nc.vector.tensor_scalar(masks, masks, 0.0, None, ALU.not_equal).then_inc(flag_ready_dve, 1)
                dve.wait_ge(flag_ready_dve, 1)
                nc.vector.tensor_reduce(flag_col[:], masks, AX.X, ALU.max).then_inc(setup_dve, 1)

            def setup_flag_value():
                dve.wait_ge(flag_ps, 1)
                nc.vector.tensor_scalar(flag_i[:], den[0:1, 0:1], 1.0, None, ALU.min).then_inc(flag_ready, 1)

            def setup_weights():
                dve.wait_ge(w1_in, 16 * 5)
                nc.vector.tensor_scalar(bq_s[:], bq_raw, SCALE, None, ALU.mult)
                last = nc.vector.tensor_scalar(wtmp, stage_w, SCALE, None, ALU.mult)
                last.then_inc(wsplit, 1)
                dve.wait_ge(wsplit, 1)
                cp(wq_h[:].rearrange("p k g c -> p k (g c)"), wtmp)
                cp(wo_h[:], stage_o).then_inc(wsplit, 1)
                dve.wait_ge(wsplit, 2)
                tt(wq_l[:].rearrange("p k g c -> p k (g c)"), wtmp,
                   wq_h[:].bitcast(F32).rearrange("p k g c -> p k (g c)"), ALU.subtract)
                tt(wo_l[:], stage_o, wo_h[:].bitcast(F32), ALU.subtract).then_inc(weights_ready, 1)

            flag_ready_dve = es.enter_context(nc.semaphore("flag_marks"))
            wsplit = es.enter_context(nc.semaphore("wsplit"))

            def z_low(i, plan, j):
                wait(dve, "zh_done", i + 1, j)
                wait(dve, "en_ps", i, 4 * j + 3)
                tt(zl[:, j], gen[:, slot(plan, f"z{j}")], zh[:, j].bitcast(F32), ALU.subtract
                   ).then_inc(sem["zl_done"], 1)

            def tva_out(i, plan, j, k):
                wait(dve, "tva_ps", i, 4 * j + k)
                wait(dve, "b_ps", i - 1, 2 * j + 1)
                wait(dve, "x2_done", i - 1, j)
                tt(ta[:, j, k], wide[:, slot(plan, f"tva{j}{k}"), 0:CW], cb_s[:], ALU.add
                   ).then_inc(sem["ta_done"], 1)

            def energy_max(i, plan, j, n):
                wait(dve, "en_ps", i, 4 * j + n)
                wait(dve, "exp_done", i - 1, 4 * j + n)
                nc.vector.tensor_reduce(negmax[:, j, n:n + 1], wide[:, slot(plan, f"en{j}{n}")],
                                        AX.X, ALU.max, negate=True).then_inc(sem["negmax_done"], 1)

            def row_inverse(i, j):
                wait(dve, "exp_done", i, 4 * j + 3)
                wait(dve, "tv_done", i - 1, 4 * j + 3)
                nc.vector.reciprocal(rowinv[:, j], rowsum[:, j]).then_inc(sem["rowinv_done"], 1)

            def layer0_out(i, plan, j):
                wait(dve, "b_ps", i, 2 * j + 1)
                first, second = slot(plan, f"b{j}0"), slot(plan, f"b{j}1")
                assert second == first + 1
                att_v = wide[:, first:first + 2].rearrange("p a (b c) -> p (a b) c", b=2)
                nc.vector.tensor_scalar(colneg[:, j], att_v[:, :, ONE], -1.0, -COL_EPS, ALU.mult, ALU.add
                                        ).then_inc(sem["colneg_done"], 1)
                wait(dve, "colneg_done", i, j)
                nc.vector.reciprocal(colinv[:, j], colneg[:, j]).then_inc(sem["colinv_done"], 1)
                wait(dve, "colinv_done", i, j)
                for m in range(KC):
                    stt(ta[:, j, m, A0:A0 + P], att_v[:, m, 0:P], colinv[:, j, m:m + 1], ta[:, j, m, A0:A0 + P],
                        ALU.mult, ALU.add).then_inc(sem["pre_done"], 1)
                wait(dve, "pre_done", i, 4 * j + 3)
                wait(dve, "x2l_done", i - 1, j)
                wait(dve, "r_ps", i - 1, j)
                stt(x2[:, :, j], ta[:, j, :, A0:A0 + P], 0.0, ta[:, j, :, X0:CW], ALU.max, ALU.add
                    ).then_inc(sem["x2_done"], 1)

            def x2_low(i, j):
                wait(dve, "x2h_done", i, j)
                wait(dve, "q_ps", i - 1, 3)
                tt(x2l[:, :, j], x2[:, :, j], x2h[:, :, j].bitcast(F32), ALU.subtract).then_inc(sem["x2l_done"], 1)

            def ctx_low(i, plan, j):
                wait(dve, "eth_done", i, j)
                wait(dve, "v_ps", i - 1, 0)
                tt(etl[:, :, j], gen[:, slot(plan, f"et{j}")].rearrange("p (k s) -> p k s", k=KC),
                   eth[:, :, j].bitcast(F32), ALU.subtract).then_inc(sem["etl_done"], 1)

            def k_low(i, plan):
                wait(dve, "kh_done", i, 0)
                wait(dve, "kb_done", i - 1, 3)
                stt(kl[:], gen[:, slot(plan, "k"), 0:2 * P].rearrange("p (j s) -> p j s", j=2), bk_s,
                    kh[:].bitcast(F32), ALU.add, ALU.subtract).then_inc(sem["kl_done"], 1)

            def q_low(q, plan, g):
                wait(dve, "qh_done", q, g)
                wait(dve, "st_ps", q - 1, 15)
                stt(ql[:, :, g], gen[:, slot(plan, f"q{g}"), 0:2 * P].rearrange("p (j l) -> p j l", j=2),
                    bq_s[:, g:g + 1], qh[:, :, g].bitcast(F32), ALU.add, ALU.subtract).then_inc(sem["ql_done"], 1)

            def score_max(q, plan, j, g, half):
                wait(dve, "mx_ps", q, 8 * j + 2 * g + half)
                if g == 0 and half == 0:
                    wait(dve, "mrow_done", q - 1, 2 * j + 1)
                at_head = g * KV + 4 * half
                nc.vector.tensor_reduce(maxima[:, j, at_head:at_head + 4],
                                        wide[:, slot(plan, f"mx{j}{g}{half}")].rearrange("p (b s) -> p b s", s=P),
                                        AX.X, ALU.max, negate=True).then_inc(sem["max_done"], 1)

            def max_split(q, j):
                wait(dve, "max_done", q, 8 * j + 7)
                wait(dve, "m_ps", q - 1, j)
                cp(mrow[:, j, 0], maxima[:, j]).then_inc(sem["mrow_done"], 1)
                wait(dve, "mrow_done", q, 2 * j)
                tt(mrow[:, j, 1], maxima[:, j], mrow[:, j, 0].bitcast(F32), ALU.subtract
                   ).then_inc(sem["mrow_done"], 1)

            def max_rows(q, plan, j):
                wait(dve, "m_ps", q, j)
                wait(dve, "st_ps", q, 8 * j - 1)
                tt(mrep[:], gen[0:64, slot(plan, f"m{j}")], gmask, ALU.mult).then_inc(sem["mrep_done"], 1)

            def weigh_out(q, j):
                wait(dve, "den_ps", q, j)
                wait(dve, "atl_done", q - 1, j)
                nc.vector.reciprocal(at[:, j], den[:]).then_inc(sem["dinv_done"], 1)
                wait(dve, "dinv_done", q, j)
                wait(dve, "o_ps", q, j)
                tt(at[:, j], outt[:], at[:, j], ALU.mult).then_inc(sem["at_done"], 1)

            def at_low(q, j):
                wait(dve, "ath_done", q, j)
                wait(dve, "wo_ps", q, j - 1)
                tt(atl[:], at[:, j].rearrange("p (g l) -> p g l", g=G), ath[:].bitcast(F32), ALU.subtract
                   ).then_inc(sem["atl_done"], 1)

            def residual_add(q, plan, j):
                wait(dve, "wo_ps", q, j)
                wait(dve, "xrb_done", q, j)
                wait(dve, "gam_done", q - 1, j)
                tt(res[:, j], gen[:, slot(plan, f"wo{j}")], xr[:, j], ALU.add).then_inc(sem["res_done"], 1)

            def row_statistics(q, j):
                wait(dve, "res_done", q, j)
                wait(dve, "ln_var", q - 1, 5)
                nc.vector.bn_stats(bns[:, j], res[:, j]).then_inc(sem["bns_done"], 1)

            def root_guess(q):
                wait(dve, "ln_var", q, 5)
                nc.vector.tensor_scalar(yi[:], nv[:, 0].bitcast(I32), -0.5, 1597463007.0, ALU.mult, ALU.add
                                        ).then_inc(sem["ln_guess"], 1)

            def iteration(i, plan, s0, s1, s2, s3):
                q = i - 1
                if s1:
                    for k in range(KC):
                        tva_out(i, plan, 0, k)
                if s2:
                    q_low(q, plan, 0)
                if s1:
                    tva_out(i, plan, 1, 0)
                    tva_out(i, plan, 1, 1)
                for g in range(G):
                    if s2:
                        if g + 1 < G:
                            q_low(q, plan, g + 1)
                        score_max(q, plan, 0, g, 0)
                        score_max(q, plan, 0, g, 1)
                    if s2 and g == G - 1:
                        max_split(q, 0)
                    if s1:
                        energy_max(i, plan, 0, g)
                        if g == 0:
                            tva_out(i, plan, 1, 2)
                            tva_out(i, plan, 1, 3)
                if s2:
                    max_rows(q, plan, 0)
                if s1:
                    energy_max(i, plan, 1, 0)
                    row_inverse(i, 0)
                for kv in range(KV):
                    if s2:
                        score_max(q, plan, 1, kv // 2, kv % 2)
                    if s3 and kv < 2:
                        row_statistics(i - 2, kv)
                    if s3 and kv == 6:
                        root_guess(i - 2)
                if s2:
                    max_split(q, 1)
                    max_rows(q, plan, 1)
                    weigh_out(q, 0)
                    at_low(q, 0)
                if s1:
                    for n in range(1, KC):
                        energy_max(i, plan, 1, n)
                    row_inverse(i, 1)
                    ctx_low(i, plan, 0)
                    ctx_low(i, plan, 1)
                if s2:
                    residual_add(q, plan, 0)
                if s1:
                    k_low(i, plan)
                if s2:
                    weigh_out(q, 1)
                    at_low(q, 1)
                if s0:
                    z_low(i, plan, 0)
                    z_low(i, plan, 1)
                if s1:
                    layer0_out(i, plan, 0)
                    x2_low(i, 0)
                    layer0_out(i, plan, 1)
                    x2_low(i, 1)
                if s2:
                    residual_add(q, plan, 1)

            iteration(-1, START, True, False, False, False)
            iteration(0, FIRST, True, True, False, False)
            setup_mask_flag()
            setup_flag_value()
            setup_weights()
            iteration(1, SECOND, True, True, True, False)
            iteration(2, FULL, True, True, True, True)
            with dve.Fori(3, PAIRS - 1) as i:
                iteration(i, FULL, True, True, True, True)
            iteration(PAIRS - 1, NEXT_TO_LAST, False, True, True, True)
            iteration(PAIRS, LAST, False, False, True, True)
            iteration(PAIRS + 1, None, False, False, False, True)


def shape_constants():
    c = np.zeros((P, C_ALL), np.float32)
    c[:, C_ID:C_ID + P] = np.eye(P)
    for k in range(KV):
        c[HD * k:HD * (k + 1), C_KVMASK + k] = 1.0
    ones = c[:, C_ONES:C_ONES + 4 * HD].reshape(P, 2, 2 * HD)
    ones[:, 0, :HD] = 1.0
    ones[:, 1, HD:] = 1.0
    c[:, C_ONES:C_ONES + 4 * HD] = ones.reshape(P, -1)
    for part in range(2):
        for g in range(G):
            row = part * G * KV + g * KV
            c[row:row + KV, C_GMASK + g * P:C_GMASK + (g + 1) * P] = 1.0
            c[row:row + KV, C_SEL:C_SEL + KV] = np.eye(KV)
    c[:, C_LN:C_ALL] = LN_CONSTANTS
    return c


def kernel(x, ctx_2048, mask_Bx1xSxS2_ff0, L0_xattn_w_qk, L0_xattn_w_v, L0_xattn_b_v, L0_xattn_w_t, L0_xattn_b_t,
           L1_xattn_Wq, L1_xattn_bq, L1_xattn_Wk, L1_xattn_bk, L1_xattn_Wv, L1_xattn_bv, L1_xattn_Wo, L1_xattn_bo,
           L1_xattn_gamma, L1_xattn_beta):
    import concourse.bacc as bacc
    from concourse.bass_utils import run_bass_kernel_spmd

    wq = np.asarray(L1_xattn_Wq).reshape(N, KV, G, HD).transpose(0, 2, 1, 3).reshape(N, N)
    wo = np.asarray(L1_xattn_Wo).reshape(KV, G, HD, N).transpose(1, 0, 2, 3).reshape(N, N)
    bq = np.asarray(L1_xattn_bq).reshape(KV, G, HD).transpose(0, 2, 1).reshape(P, G)
    columns = np.concatenate([bq] + [np.asarray(b).reshape(P, 1) for b in (L1_xattn_bk, L1_xattn_bv, L0_xattn_b_v)], 1)
    arrays = {
        "in_x": x, "in_ctx": ctx_2048, "in_mask": mask_Bx1xSxS2_ff0, "in_w_qk": L0_xattn_w_qk, "in_w_v": L0_xattn_w_v,
        "in_w_t": L0_xattn_w_t, "in_b_t": L0_xattn_b_t, "in_Wq": wq, "in_Wk": L1_xattn_Wk, "in_Wv": L1_xattn_Wv,
        "in_Wo": wo, "in_bo": L1_xattn_bo, "in_gamma": L1_xattn_gamma, "in_beta": L1_xattn_beta,
        "in_columns": columns, "shape_constants": shape_constants(),
    }
    arrays = {n: np.ascontiguousarray(a) for n, a in arrays.items()}
    nc = bacc.Bacc("TRN2", target_bir_lowering=False, num_devices=1)
    args = [nc.dram_tensor(n, a.shape, mybir.dt.from_np(a.dtype), kind="ExternalInput").ap() for n, a in arrays.items()]
    out = nc.dram_tensor("out_x", (B, P, N), F32, kind="ExternalOutput").ap()
    build_xattn(nc, *args, out)
    r = run_bass_kernel_spmd(nc, [arrays], core_ids=[0])
    return r.results[0]["out_x"]
```

```python
from contextlib import ExitStack

import numpy as np

import concourse.bass as bass
from concourse import mybir

F32 = mybir.dt.float32
F32R = mybir.dt.float32r
I32 = mybir.dt.int32
ALU = mybir.AluOpType
ACT = mybir.ActivationFunctionType
AX = mybir.AxisListType

P = 128
B = 32
PAIRS = B // 2
N = 512
KC = N // P
KV = 8
G = 4
HD = 16
SCALE = 0.25
COL_EPS = 1e-7
LN_EPS = 1e-6

ONE = P
A0 = P + 2
X0 = A0 + P
CW = X0 + P
BW = P + 2

MROWS = 2 * G * 2

C_ID = 0
C_KVMASK = C_ID + P
C_ONES = C_KVMASK + KV
C_GMASK = C_ONES + 2 * 2 * HD
C_SEL = C_GMASK + G
C_ODD = C_SEL + KV
C_MODD = C_ODD + 2
C_LN = C_MODD + 2
LN_CONSTANTS = (1.0 / N, LN_EPS, 0.25, -0.5, 1.5)
C_ALL = C_LN + len(LN_CONSTANTS)

GEN_USES = (
    [(f"q{g}", 2) for g in range(G)]
    + [("m0", 2), ("r0", 2), ("r1", 2), ("m1", 2)]
    + [("et0", 1), ("et1", 1), ("wo0", 2), ("k", 1), ("v", 1), ("z0", 0), ("z1", 0)]
    + [("vt0", 1), ("vt1", 1), ("wo1", 2)]
)
WIDE_USES = (
    [(f"tva0{k}", 1) for k in range(KC)]
    + [("en00", 1), ("en01", 1), ("mx000", 2), ("mx001", 2), ("en02", 1), ("mx010", 2), ("mx011", 2)]
    + [("tva10", 1), ("tva11", 1), ("mx020", 2), ("mx021", 2), ("tva12", 1), ("tva13", 1)]
    + [("mx030", 2), ("mx031", 2), ("en03", 1), ("en10", 1), ("mx100", 2), ("mx101", 2)]
    + [u for kv in range(6) for u in ((f"st0{kv}", 2), (f"mx1{(kv + 2) // 2}{kv % 2}", 2))]
    + [("st06", 2), ("st07", 2)]
    + [("en11", 1)] + [(f"st1{kv}", 2) for kv in range(4)]
    + [("en12", 1), ("en13", 1)] + [(f"st1{kv}", 2) for kv in range(4, KV)]
    + [(f"b{j}{h}", 1) for j in range(2) for h in range(2)]
)
GEN_SLOTS, WIDE_SLOTS = 2, 4


def ring(uses, slots, stages, stages_before):
    now = [n for n, s in uses if s in stages]
    before = [n for n, s in uses if s in stages_before]
    assert len(now) % slots == 0 and len(before) % slots == 0
    plan = {}
    for at, name in enumerate(now):
        if at >= slots:
            plan[name] = (at % slots, now[at - slots], 0)
        elif before:
            plan[name] = (at % slots, before[len(before) - slots + at], 1)
        else:
            plan[name] = (at % slots, None, 0)
    return plan


def build_xattn(nc, x, ctx, mask, w_qk, w_v, w_t, b_t, Wq, Wk, Wv, Wo, bo, gamma, beta, columns, consts, out):
    es = ExitStack()
    with es:
        def sb(name, shape, dt=F32):
            return es.enter_context(nc.sbuf_tensor(name, shape, dt))

        def ps(name, shape):
            return es.enter_context(nc.psum_tensor(name, shape, F32))

        cst = sb("cst", [P, C_ALL])
        ident = cst[:, C_ID:C_ID + P]
        kvmask = cst[:, C_KVMASK:C_KVMASK + KV]
        ones_eo = cst[:, C_ONES:C_ONES + 4 * HD].rearrange("p (o c) -> p o c", o=2)
        gmask = cst[0:64, C_GMASK:C_GMASK + G]
        parity = cst[:, C_ODD:C_ODD + 2]
        row_parity = cst[96:96 + MROWS, C_MODD:C_MODD + 2]
        sel_f = cst[0:64, C_SEL:C_SEL + KV]
        per_n, ln_eps, quarter, minus_half, three_halves = (
            cst[:, c:c + 1].broadcast_to([P, 2]) for c in range(C_LN, C_ALL))
        sel = sb("sel", [2 * G * KV, KV], F32R)
        ident_r = sb("ident_r", [P, P], F32R)
        cols = sb("cols", [P, G + 3])
        bq_raw, bk_s, bv_s, b0_s = cols[:, 0:G], cols[:, G:G + 1], cols[:, G + 1:G + 2], cols[:, G + 2:G + 3]
        gram_h = sb("gram_h", [P, P], F32R)
        gram_l = sb("gram_l", [P, P], F32R)
        cw_h = sb("cw_h", [P, CW], F32R)
        cw_l = sb("cw_l", [P, CW], F32R)
        cb_s = sb("cb_s", [P, CW])
        att = sb("att", [P, 2, KC, N])
        setup = att[:].rearrange("p a b n -> p (a b n)")
        cw_s = setup[:, 4 * N:4 * N + CW]
        wqk_s, wv_s, wt_s, wtT_s = (setup[:, 5 * N + n * P:5 * N + (n + 1) * P] for n in range(4))
        late = sb("late", [P, 2, 2, N])
        stage_w = late[:].rearrange("p a b n -> p (a b) n")
        wq_h = sb("wq_h", [P, KC, G, P], F32R)
        wq_l = sb("wq_l", [P, KC, G, P], F32R)
        wkv_h = sb("wkv_h", [P, 2, KC, P], F32R)
        wkv_l = sb("wkv_l", [P, 2, KC, P], F32R)
        wo_h = sb("wo_h", [P, G, N], F32R)
        wo_l = sb("wo_l", [P, G, N], F32R)
        bq_s = sb("bq_s", [P, G])
        bo_b = sb("bo_b", [P, N])
        gamma_b = sb("gamma_b", [P, N])
        beta_b = sb("beta_b", [P, N])
        mask_sums = sb("mask_sums", [P, 2])
        flag_col = sb("flag_col", [P, 2])
        flag_i = sb("flag_i", [1, 1], I32)

        xs = sb("xs", [P, 2, N])
        ys = sb("ys", [P, 2, N])
        mk = sb("mk", [P, 2, P])
        xh = sb("xh", [P, 2, N], F32R)
        xl = sb("xl", [P, 2, N], F32R)
        yh = sb("yh", [P, 2, N], F32R)
        yl = sb("yl", [P, 2, N], F32R)
        zh = sb("zh", [P, 2, N], F32R)
        zl = sb("zl", [P, 2, N], F32R)
        ta = sb("ta", [P, 2, KC, CW])
        negmax = sb("negmax", [P, 2, KC])
        rowsum = sb("rowsum", [P, 2, KC])
        rowinv = sb("rowinv", [P, 2, KC])
        colneg = sb("colneg", [P, 2, KC])
        colinv = sb("colinv", [P, 2, KC])
        x2 = sb("x2", [P, KC, 2, P])
        x2h = sb("x2h", [P, KC, 2, P], F32R)
        x2l = sb("x2l", [P, KC, 2, P], F32R)
        eth, etl = x2h, x2l
        kh = sb("kh", [P, 2, P], F32R)
        kl = sb("kl", [P, 2, P], F32R)
        kbh = sb("kbh", [P, 2, KV, P], F32R)
        kpl = sb("kpl", [P, 2, 2, P], F32R)
        qstack = sb("qstack", [P, KV // 2, 2, G, P], F32R)
        kstack = sb("kstack", [P, 2, KV, P], F32R)
        vts = sb("vts", [P, 2, P])
        v2 = sb("v2", [P, 2, KV, 2 * HD])
        qh = sb("qh", [P, 2, G, P], F32R)
        ql = sb("ql", [P, 2, G, P], F32R)
        maxima = sb("maxima", [P, 2, G * KV])
        mrow = sb("mrow", [P, 2, KV // 2, 2, 2 * G], F32R)
        mrep = sb("mrep", [2 * G * KV, G, P], F32R)
        prob = sb("prob", [P, KV, G * P])
        stage_o = prob[:, 0:G]
        stage_kv = x2[:].rearrange("p a j l -> p (a j l)").rearrange("p (w k c) -> p w k c", w=2, k=KC)
        all_masks = prob[:].rearrange("p k n -> p (k n)")
        res, outb = late[:, 0], late[:, 1]
        at = sb("at", [P, N])
        ath = sb("ath", [P, G, P], F32R)
        atl = sb("atl", [P, G, P], F32R)
        bns = sb("bns", [P, 2, 6])
        mv = sb("mv", [P, 2, 2])
        nv = sb("nv", [P, 8, 2])
        yi = sb("yi", [P, 2], I32)

        wide = ps("wide", [P, WIDE_SLOTS, N])
        gen = ps("gen", [P, GEN_SLOTS, N])
        den = ps("den", [P, N])
        outt = ps("outt", [P, N])

        SEMS = dict(
            xh_done=2, x_split=2, yh_done=2, y_split=2, kb_done=2, kp_done=1, ta_done=4, tv_done=2, xrb_done=2, gam_done=2, out_ready=2, ln_var=6, ln_step=13,
            z_ps=2, tva_ps=8, et_ps=2, k_ps=1, v_ps=1, vt_ps=2, en_ps=8, b_ps=4,
            q_ps=4, r_ps=2, mx_ps=16, m_ps=2, st_ps=16, den_ps=2, o_ps=2, wo_ps=2,
            zh_done=2, exp_done=8, ta_raw=8, eth_done=2, kh_done=1, vts_done=1, v2_done=4, x2h_done=2,
            qh_done=4, xr_done=2, prob_done=16, ath_done=2, nrm_done=2,
            zl_done=2, negmax_done=8, rowinv_done=2, colneg_done=2, colinv_done=2, pre_done=8,
            x2_done=2, x2l_done=2, etl_done=2, kl_done=1, ql_done=4, max_done=16, mrow_done=4, mrep_done=2, dinv_done=2,
            at_done=2, atl_done=2, res_done=2, bns_done=2, ln_sums=1, ln_guess=1,
        )
        sem = {k: es.enter_context(nc.semaphore(k)) for k in SEMS}
        x_in = es.enter_context(nc.semaphore("x_in"))
        y_in = es.enter_context(nc.semaphore("y_in"))
        mask_in = es.enter_context(nc.semaphore("mask_in"))
        qstack_in = [es.enter_context(nc.semaphore(f"qstack_in{p}")) for p in range(KV // 2)]
        kstack_in = es.enter_context(nc.semaphore("kstack_in"))
        out_sem = [es.enter_context(nc.semaphore(f"out_done{j}")) for j in range(2)]
        cst_in = es.enter_context(nc.semaphore("constants_in"))
        wqk_in = es.enter_context(nc.semaphore("wqk_in"))
        w0_in = es.enter_context(nc.semaphore("layer0_weights_in"))
        wkv_in = es.enter_context(nc.semaphore("wkv_in"))
        wq_in = es.enter_context(nc.semaphore("wq_in"))
        wo_in = es.enter_context(nc.semaphore("wo_in"))
        rows_in = es.enter_context(nc.semaphore("rows_in"))
        allmask_in = es.enter_context(nc.semaphore("allmask_in"))
        setup_pe = es.enter_context(nc.semaphore("setup_pe"))
        setup_dve = es.enter_context(nc.semaphore("setup_dve"))
        cw_ready = es.enter_context(nc.semaphore("cw_ready"))
        wkv_high = es.enter_context(nc.semaphore("wkv_high"))
        wkv_ready = es.enter_context(nc.semaphore("wkv_ready"))
        wq_high = es.enter_context(nc.semaphore("wq_high"))
        wq_ready = es.enter_context(nc.semaphore("wq_ready"))
        wo_high = es.enter_context(nc.semaphore("wo_high"))
        wo_ready = es.enter_context(nc.semaphore("wo_ready"))
        mask_sums_done = es.enter_context(nc.semaphore("mask_sums_done"))
        flag_marks = es.enter_context(nc.semaphore("flag_marks"))
        flag_ps = es.enter_context(nc.semaphore("flag_ps"))
        last_rows = es.enter_context(nc.semaphore("last_rows"))
        flag_ready = es.enter_context(nc.semaphore("flag_ready"))
        zeros_ready = es.enter_context(nc.semaphore("zeros_ready"))

        def wait(eng, name, pair, n):
            value = pair * SEMS[name] + (n + 1)
            if isinstance(value, int) and value <= 0:
                return
            eng.wait_ge(sem[name], value)

        RELEASE = {}
        for j in range(2):
            RELEASE[f"z{j}"] = ("zl_done", j, 0)
            RELEASE[f"et{j}"] = ("etl_done", j, 1)
            RELEASE[f"vt{j}"] = ("v2_done", 2 * j + 1, 1)
            RELEASE[f"r{j}"] = ("xr_done", j, 2)
            RELEASE[f"m{j}"] = ("mrep_done", j, 2)
            RELEASE[f"wo{j}"] = ("res_done", j, 2)
            for k in range(4):
                RELEASE[f"tva{j}{k}"] = ("ta_raw", 4 * j + k, 1)
                RELEASE[f"en{j}{k}"] = ("exp_done", 4 * j + k, 1)
            for h in range(2):
                RELEASE[f"b{j}{h}"] = ("pre_done", 4 * j + 2 * h + 1, 1)
            for kv in range(KV):
                RELEASE[f"mx{j}{kv // 2}{kv % 2}"] = ("max_done", 8 * j + kv, 2)
                RELEASE[f"st{j}{kv}"] = ("prob_done", 8 * j + kv, 2)
        for g in range(G):
            RELEASE[f"q{g}"] = ("ql_done", g, 2)
        RELEASE["k"] = ("kl_done", 0, 1)
        RELEASE["v"] = ("vts_done", 0, 1)

        def plans(stages, before):
            return {**ring(GEN_USES, GEN_SLOTS, stages, before), **ring(WIDE_USES, WIDE_SLOTS, stages, before)}

        def slot(plan, name):
            return plan[name][0]

        def wait_slot(eng, plan, name, i):
            _, prev, back = plan[name]
            if prev is not None:
                signal, n, stage = RELEASE[prev]
                wait(eng, signal, i - back + 1 - stage, n)

        START = plans((0,), ())
        FIRST = plans((0, 1), (0,))
        SECOND = plans((0, 1, 2), (0, 1))
        FULL = plans((0, 1, 2), (0, 1, 2))
        NEXT_TO_LAST = plans((1, 2), (0, 1, 2))
        LAST = plans((2,), (1, 2))

        block = es.enter_context(nc.Block())

        @block.sync
        def _(sp):
            def load_x(pair):
                sp.dma_start(xs[:], x[bass.ts(pair, 2)].rearrange("b c n -> c b n")).then_inc(x_in, 16)

            def load_y(pair):
                sp.dma_start(ys[:], ctx[bass.ts(pair, 2)].rearrange("b c n -> c b n")).then_inc(y_in, 16)

            def load_mask(pair):
                sp.dma_start(mk[:], mask[bass.ts(pair, 2)].rearrange("b o l s -> l (b o) s")).then_inc(mask_in, 16)

            def store(pair, j):
                sp.dma_start(out[bass.ds(pair * 2 + j, 1)].rearrange("b l h -> l b h"),
                             outb[:, j:j + 1, :]).then_inc(out_sem[j], 16)

            def stack_q(q):
                wait(sp, "ql_done", q, G - 1)
                wait(sp, "st_ps", q - 1, 15)
                for p in range(KV // 2):
                    for part, src in enumerate((qh, ql, qh)):
                        sp.dma_start(qstack[32 * part:32 * part + 32, p].bitcast(F32),
                                     src[32 * p:32 * p + 32].bitcast(F32)).then_inc(qstack_in[p], 16)

            def stack_maxima(q):
                wait(sp, "mrep_done", q, 1)
                for p in range(KV // 2):
                    sp.dma_start(qstack[96:96 + MROWS, p, 1].bitcast(F32),
                                 mrep[MROWS * p:MROWS * (p + 1)].bitcast(F32)).then_inc(qstack_in[p], 16)

            def stack_k(i):
                wait(sp, "kb_done", i, 1)
                wait(sp, "kp_done", i, 0)
                wait(sp, "st_ps", i - 1, 15)
                for p in range(KV // 2):
                    rows, heads = slice(32 * p, 32 * p + 32), slice(2 * p, 2 * p + 2)
                    for part, src in enumerate((kbh[rows, :, heads], kbh[rows, :, heads], kpl[rows])):
                        sp.dma_start(kstack[32 * part:32 * part + 32, :, heads].bitcast(F32),
                                     src.bitcast(F32)).then_inc(kstack_in, 16)

            def iteration(i, load_next, s1, s2, s3, setup=False):
                if load_next:
                    wait(sp, "x_split", i, 1)
                    load_x(i + 1)
                if setup:
                    sp.dma_start(stage_w, Wq.rearrange("(k p) n -> p k n", p=P)).then_inc(wq_in, 16)
                    for dst, src in ((bo_b, bo), (gamma_b, gamma), (beta_b, beta)):
                        sp.dma_start(dst[:], src.partition_broadcast(P)).then_inc(rows_in, 16)
                    sp.wait_ge(mask_sums_done, 1)
                    sp.dma_start(stage_o, Wo.rearrange("(g p) n -> p g n", g=G)).then_inc(wo_in, 16)
                if s2:
                    stack_q(i - 1)
                    stack_maxima(i - 1)
                if s3:
                    for j in range(2):
                        if j == 1 and isinstance(i, int) and i == PAIRS + 1:
                            sp.wait_ge(last_rows, 3)
                        else:
                            wait(sp, "out_ready", i - 2, j)
                        store(i - 2, j)
                if s1:
                    if not isinstance(i, int) or i > 0:
                        sp.wait_ge(mask_in, i * 16)
                    wait(sp, "st_ps", i - 1, 15)
                    load_mask(i)
                if load_next:
                    wait(sp, "y_split", i, 1)
                    wait(sp, "et_ps", i, 1)
                    load_y(i + 1)
                if s1:
                    stack_k(i)

            sp.dma_start(wqk_s, w_qk).then_inc(wqk_in, 16)
            load_x(0)
            sp.dma_start(cst[:], consts).then_inc(cst_in, 16)
            for dst, src in ((wt_s, w_t), (wv_s, w_v), (cols[:], columns),
                             (cb_s[:, A0:A0 + P], b_t.partition_broadcast(P))):
                sp.dma_start(dst, src).then_inc(w0_in, 16)
            load_y(0)
            sp.dma_start(stage_kv[:, 0], Wk.rearrange("(k p) n -> p k n", p=P)).then_inc(wkv_in, 16)
            sp.dma_start(stage_kv[:, 1], Wv.rearrange("(k p) n -> p k n", p=P)).then_inc(wkv_in, 16)
            sp.dma_start(all_masks, mask.rearrange("b o l s -> (b o l s)").rearrange("(p f) -> p f", p=P)
                         ).then_inc(allmask_in, 16)
            iteration(0, True, True, False, False, setup=True)
            iteration(1, True, True, True, False)
            iteration(2, True, True, True, True)
            with sp.Fori(3, PAIRS - 1) as i:
                iteration(i, True, True, True, True)
            iteration(PAIRS - 1, False, True, True, True)
            iteration(PAIRS, False, False, True, True)
            iteration(PAIRS + 1, False, False, False, True)
            for j in range(2):
                sp.wait_ge(out_sem[j], 16 * PAIRS)

        @block.gpsimd
        def _(pool):
            one_col = ones_eo[:, 0, 0:1].broadcast_to([P, N])
            nc.gpsimd.memset(v2[:], 0.0).then_inc(zeros_ready, 1)

            def split_x(i, j):
                if j == 0:
                    pool.wait_ge(x_in, i * 16 + 16)
                wait(pool, "tva_ps", i - 1, 4 * j + 3)
                nc.gpsimd.tensor_tensor(xh[:, j], xs[:, j], one_col, ALU.mult).then_inc(sem["xh_done"], 1)
                wait(pool, "xh_done", i, j)
                nc.gpsimd.tensor_tensor(xl[:, j], xs[:, j], xh[:, j].bitcast(F32), ALU.subtract
                                        ).then_inc(sem["x_split"], 1)

            def split_y(i, j):
                if j == 0:
                    pool.wait_ge(y_in, i * 16 + 16)
                wait(pool, "en_ps", i - 1, 4 * j + 3)
                nc.gpsimd.tensor_tensor(yh[:, j], ys[:, j], one_col, ALU.mult).then_inc(sem["yh_done"], 1)
                wait(pool, "yh_done", i, j)
                nc.gpsimd.tensor_tensor(yl[:, j], ys[:, j], yh[:, j].bitcast(F32), ALU.subtract
                                        ).then_inc(sem["y_split"], 1)

            def spread_k(i):
                wait(pool, "kl_done", i, 0)
                wait(pool, "st_ps", i - 1, 15)
                for j in range(2):
                    shape = [P, KV, P]
                    nc.gpsimd.tensor_tensor(kbh[:, j], kh[:, j].bitcast(F32).unsqueeze(1).broadcast_to(shape),
                                            kvmask.unsqueeze(2).broadcast_to(shape), ALU.mult
                                            ).then_inc(sem["kb_done"], 1)
                shape = [P, 2, 2, P]
                nc.gpsimd.tensor_tensor(kpl[:], kl[:].bitcast(F32).unsqueeze(2).broadcast_to(shape),
                                        parity.unsqueeze(1).unsqueeze(3).broadcast_to(shape), ALU.mult
                                        ).then_inc(sem["kp_done"], 1)

            def add_bias(i, j, h):
                wait(pool, "ta_raw", i, 4 * j + 2 * h + 1)
                part = ta[:, j, 2 * h:2 * h + 2]
                nc.gpsimd.tensor_tensor(part, part, cb_s[:].unsqueeze(1).broadcast_to([P, 2, CW]), ALU.add
                                        ).then_inc(sem["ta_done"], 1)

            def scale_values(i, j):
                wait(pool, "rowinv_done", i, j)
                wait(pool, "ta_done", i, 2 * j + 1)
                part = ta[:, j, :, 0:BW]
                nc.gpsimd.tensor_tensor(part, part, rowinv[:, j].unsqueeze(2).broadcast_to([P, KC, BW]), ALU.mult
                                        ).then_inc(sem["tv_done"], 1)

            def residual_bias(q, j):
                wait(pool, "xr_done", q, j)
                nc.gpsimd.tensor_tensor(res[:, j], res[:, j], bo_b[:], ALU.add).then_inc(sem["xrb_done"], 1)

            def scale_shift(q, j):
                wait(pool, "nrm_done", q, j)
                nc.gpsimd.tensor_tensor(outb[:, j], outb[:, j], gamma_b[:], ALU.mult).then_inc(sem["gam_done"], 1)
                wait(pool, "gam_done", q, j)
                nc.gpsimd.tensor_tensor(outb[:, j], outb[:, j], beta_b[:], ALU.add).then_inc(sem["out_ready"], 1)

            def variance(q):
                step = [0]

                def link(ins):
                    ins.then_inc(sem["ln_var"], 1)
                    wait(pool, "ln_var", q, step[0])
                    step[0] += 1

                op = nc.gpsimd.tensor_tensor
                v, t, dev = nv[:, 0], nv[:, 4], nv[:, 5]
                wait(pool, "bns_done", q, 1)
                wait(pool, "nrm_done", q - 1, 1)
                op(mv[:], bns[:, :, 1:3], bns[:, :, 4:6], ALU.add)
                link(op(dev, bns[:, :, 1], bns[:, :, 4], ALU.subtract))
                op(t, mv[:, :, 1], per_n, ALU.mult)
                link(op(dev, dev, dev, ALU.mult))
                op(t, t, ln_eps, ALU.add)
                link(op(dev, dev, quarter, ALU.mult))
                link(op(v, t, dev, ALU.add))
                link(op(nv[:, 1], v, minus_half, ALU.mult))
                link(op(nv[:, 7], mv[:, :, 0], minus_half, ALU.mult))

            def newton_root(q):
                step = [0]

                def link(ins):
                    ins.then_inc(sem["ln_step"], 1)
                    wait(pool, "ln_step", q, step[0])
                    step[0] += 1

                op = nc.gpsimd.tensor_tensor
                half, t, dev, shift = nv[:, 1], nv[:, 4], nv[:, 5], nv[:, 7]
                wait(pool, "ln_guess", q, 0)
                for old, new in ((yi[:].bitcast(F32), nv[:, 2]), (nv[:, 2], nv[:, 3]), (nv[:, 3], nv[:, 6])):
                    link(op(t, old, old, ALU.mult))
                    link(op(dev, t, half, ALU.mult))
                    link(op(t, dev, three_halves, ALU.add))
                    link(op(new, t, old, ALU.mult))
                link(op(shift, shift, nv[:, 6], ALU.mult))

            def iteration(i, s1, s2, s3, split_next):
                if s3:
                    variance(i - 2)
                if split_next:
                    split_x(i + 1, 0)
                if s3:
                    newton_root(i - 2)
                if s1:
                    for j in range(2):
                        add_bias(i, j, 0)
                        add_bias(i, j, 1)
                if split_next:
                    split_x(i + 1, 1)
                if s2:
                    residual_bias(i - 1, 0)
                    residual_bias(i - 1, 1)
                if s3:
                    scale_shift(i - 2, 0)
                if s1:
                    scale_values(i, 0)
                if s3 and (s1 or s2):
                    scale_shift(i - 2, 1)
                if s1:
                    scale_values(i, 1)
                    spread_k(i)
                if split_next:
                    split_y(i + 1, 0)
                    split_y(i + 1, 1)

            pool.wait_ge(cst_in, 16)
            for j in range(2):
                split_x(0, j)
            for j in range(2):
                split_y(0, j)
            iteration(0, True, False, False, True)
            pool.wait_ge(wo_high, 1)
            nc.gpsimd.tensor_tensor(wo_l[:], stage_o, wo_h[:].bitcast(F32), ALU.subtract).then_inc(wo_ready, 1)
            pool.wait_ge(rows_in, 16 * 3)
            iteration(1, True, True, False, True)
            iteration(2, True, True, True, True)
            with pool.Fori(3, PAIRS - 1) as i:
                iteration(i, True, True, True, True)
            iteration(PAIRS - 1, True, True, True, False)
            iteration(PAIRS, False, True, True, False)
            iteration(PAIRS + 1, False, False, True, False)

        @block.tensor
        def _(pe):
            mm = nc.tensor.matmul

            pe.wait_ge(wqk_in, 16)
            mm(gen[:, 0, 0:P], wqk_s, wqk_s, start=True, stop=True)
            pe.wait_ge(w0_in, 16 * 4)
            pe.wait_ge(cst_in, 16)
            nc.tensor.transpose(den[:, 0:P], wt_s, ident).then_inc(setup_pe, 1)
            pe.wait_ge(setup_dve, 2)
            mm(wide[:, 0, 0:P], wv_s, wtT_s, start=True, stop=True)
            mm(outt[:, 0:P], b0_s.broadcast_to([P, P]), wtT_s, start=True, stop=True).then_inc(setup_pe, 1)
            pe.wait_ge(setup_dve, 3)

            def z_project(i, plan, j):
                wait(pe, "x_split", i + 1, j)
                wait_slot(pe, plan, f"z{j}", i)
                o = gen[:, slot(plan, f"z{j}")]
                mm(o, gram_h[:], xh[:, j], start=True, stop=False)
                mm(o, gram_h[:], xl[:, j], start=False, stop=False)
                mm(o, gram_l[:], xh[:, j], start=False, stop=True).then_inc(sem["z_ps"], 1)

            def tva_project(i, plan, j, k):
                name = f"tva{j}{k}"
                wait_slot(pe, plan, name, i)
                o = wide[:, slot(plan, name)]
                a, b = xh[:, j, bass.ts(k, P)], xl[:, j, bass.ts(k, P)]
                mm(o[:, 0:CW], a, cw_h[:], start=True, stop=False)
                mm(o[:, 0:CW], b, cw_h[:], start=False, stop=False)
                mm(o[:, 0:X0], a, cw_l[:, 0:X0], start=False, stop=True).then_inc(sem["tva_ps"], 1)

            def energy(i, plan, j, n):
                name = f"en{j}{n}"
                if n == 0:
                    wait(pe, "zl_done", i, j)
                    wait(pe, "y_split", i, j)
                wait_slot(pe, plan, name, i)
                o = wide[:, slot(plan, name)]
                a, b = yh[:, j, bass.ts(n, P)], yl[:, j, bass.ts(n, P)]
                mm(o, a, zh[:, j], start=True, stop=False)
                mm(o, a, zl[:, j], start=False, stop=False)
                mm(o, b, zh[:, j], start=False, stop=True).then_inc(sem["en_ps"], 1)

            def attend(i, plan, j, h):
                name = f"b{j}{h}"
                if h == 0:
                    wait(pe, "tv_done", i, j)
                wait_slot(pe, plan, name, i)
                for half in range(2):
                    m = 2 * h + half
                    o = wide[:, slot(plan, name), half * 256:half * 256 + BW]
                    for n in range(KC):
                        last = mm(o, att[:, j, n, bass.ts(m, P)], ta[:, j, n, 0:BW], start=n == 0, stop=n == KC - 1)
                last.then_inc(sem["b_ps"], 1)

            def ctx_transpose(i, plan, j):
                name = f"et{j}"
                if j == 0:
                    pe.wait_ge(y_in, i * 16 + 16)
                wait_slot(pe, plan, name, i)
                for k in range(KC):
                    last = nc.tensor.transpose(gen[:, slot(plan, name), bass.ts(k, P)], ys[:, j, bass.ts(k, P)], ident)
                last.then_inc(sem["et_ps"], 1)

            def kv_project(i, plan, name, n, done):
                wait(pe, "etl_done", i, 1)
                wait_slot(pe, plan, name, i)
                o = gen[:, slot(plan, name), 0:2 * P]
                for k in range(KC):
                    mm(o, wkv_h[:, n, k], eth[:, k], start=k == 0, stop=False)
                    mm(o, wkv_h[:, n, k], etl[:, k], start=False, stop=False)
                    last = mm(o, wkv_l[:, n, k], eth[:, k], start=False, stop=k == KC - 1)
                last.then_inc(sem[done], 1)

            def v_transpose(i, plan, j):
                name = f"vt{j}"
                wait(pe, "vts_done", i, 0)
                wait_slot(pe, plan, name, i)
                nc.tensor.transpose(gen[:, slot(plan, name), 0:P], vts[:, j], ident).then_inc(sem["vt_ps"], 1)

            def q_project(q, plan, i, g):
                name = f"q{g}"
                if g == 0:
                    wait(pe, "x2l_done", q, 1)
                wait_slot(pe, plan, name, i)
                o = gen[:, slot(plan, name), 0:2 * P]
                for k in range(KC):
                    mm(o, wq_h[:, k, g], x2h[:, k], start=k == 0, stop=False)
                    mm(o, wq_h[:, k, g], x2l[:, k], start=False, stop=False)
                    last = mm(o, wq_l[:, k, g], x2h[:, k], start=False, stop=k == KC - 1)
                last.then_inc(sem["q_ps"], 1)

            def residual_transpose(q, plan, i, j):
                name = f"r{j}"
                wait(pe, "x2_done", q, j)
                wait_slot(pe, plan, name, i)
                for k in range(KC):
                    last = nc.tensor.transpose(gen[:, slot(plan, name), bass.ts(k, P)], x2[:, k, j], ident)
                last.then_inc(sem["r_ps"], 1)

            def max_scores(q, plan, i, j, g, half, masked):
                name = f"mx{j}{g}{half}"
                if half == 0:
                    wait(pe, "ql_done", q, g)
                if g == 0 and half == 0:
                    wait(pe, "kb_done", q, j)
                wait_slot(pe, plan, name, i)
                o = wide[:, slot(plan, name)]
                last = mm(o, qh[:, j, g], kbh[:, j, 4 * half:4 * half + 4], start=True, stop=not masked)
                if masked:
                    last = mm(o, ident, mk[:, j].unsqueeze(1).broadcast_to([P, 4, P]), start=False, stop=True)
                last.then_inc(sem["mx_ps"], 1)

            def max_spread(q, plan, i, j):
                name = f"m{j}"
                wait(pe, "mrow_done", q, 2 * j + 1)
                wait_slot(pe, plan, name, i)
                mm(gen[0:64, slot(plan, name)], mrow[:, j].rearrange("p a t m -> p (a t m)"), ident_r[:].unsqueeze(1).broadcast_to([P, G, P]), start=True, stop=True).then_inc(sem["m_ps"], 1)

            def scores(q, plan, i, j, kv, masked):
                name = f"st{j}{kv}"
                if kv == 0:
                    wait(pe, "mrep_done", q, j)
                if j == 0 and kv == 0:
                    pe.wait_ge(kstack_in, (q + 1) * 16 * 3 * (KV // 2))
                if kv % 2 == 0:
                    pe.wait_ge(qstack_in[kv // 2], q * 16 * 4 + 16 * (3 + j))
                wait_slot(pe, plan, name, i)
                o = wide[:, slot(plan, name)]
                rows = 96 + j * MROWS
                last = mm(o, kstack[0:rows, j, kv], qstack[0:rows, kv // 2, j], start=True, stop=j == 1 and not masked)
                if j == 0:
                    last = mm(o, sel[:, kv:kv + 1].broadcast_to([2 * G * KV, P]), mrep[:], start=False,
                              stop=not masked)
                if masked:
                    last = mm(o, mk[:, j], ident.unsqueeze(1).broadcast_to([P, G, P]), start=False, stop=True)
                last.then_inc(sem["st_ps"], 1)

            def weigh(q, j, dst, operand, done):
                wait(pe, "prob_done", q, 8 * j + 7)
                wait(pe, "at_done", q, j - 1)
                for odd in range(2):
                    for p in range(KV // 2):
                        last = mm(dst[32 * p:32 * p + 32, :], operand(2 * p + odd, odd), prob[:, 2 * p + odd],
                                  start=odd == 0, stop=odd == 1, tile_position=(0, 32 * p))
                last.then_inc(sem[done], 1)

            def denominators(q, j):
                weigh(q, j, den, lambda kv, odd: ones_eo[:, odd], "den_ps")

            def values(q, j):
                if j == 0:
                    wait(pe, "v2_done", q, 3)
                weigh(q, j, outt, lambda kv, odd: v2[:, j, kv], "o_ps")

            def out_project(q, plan, i, j):
                name = f"wo{j}"
                if isinstance(i, int) and i == 1 and j == 0:
                    pe.wait_ge(wo_ready, 1)
                wait(pe, "atl_done", q, j)
                wait_slot(pe, plan, name, i)
                o = gen[:, slot(plan, name)]
                for g in range(G):
                    mm(o, ath[:, g], wo_h[:, g], start=g == 0, stop=False)
                    mm(o, ath[:, g], wo_l[:, g], start=False, stop=False)
                    last = mm(o, atl[:, g], wo_h[:, g], start=False, stop=g == G - 1)
                last.then_inc(sem["wo_ps"], 1)

            def iteration(i, plan, s0, s1, s2, masked):
                q = i - 1

                def both_max_scores(j, g):
                    max_scores(q, plan, i, j, g, 0, masked)
                    max_scores(q, plan, i, j, g, 1, masked)

                if s1:
                    for k in range(KC):
                        tva_project(i, plan, 0, k)
                for n in range(3):
                    if s2:
                        q_project(q, plan, i, n)
                    if s1:
                        energy(i, plan, 0, n)
                    if s2 and n > 0:
                        both_max_scores(0, n - 1)
                if s2:
                    q_project(q, plan, i, 3)
                for g in range(2, G):
                    if s1:
                        tva_project(i, plan, 1, 2 * g - 4)
                        tva_project(i, plan, 1, 2 * g - 3)
                    if s2:
                        both_max_scores(0, g)
                if s1:
                    energy(i, plan, 0, 3)
                    energy(i, plan, 1, 0)
                if s2:
                    max_spread(q, plan, i, 0)
                    residual_transpose(q, plan, i, 0)
                    both_max_scores(1, 0)
                    for kv in range(6):
                        scores(q, plan, i, 0, kv, masked)
                        if kv == 0:
                            residual_transpose(q, plan, i, 1)
                        max_scores(q, plan, i, 1, (kv + 2) // 2, kv % 2, masked)
                    scores(q, plan, i, 0, 6, masked)
                    scores(q, plan, i, 0, 7, masked)
                if s1:
                    energy(i, plan, 1, 1)
                if s2:
                    max_spread(q, plan, i, 1)
                    denominators(q, 0)
                    values(q, 0)
                    for kv in range(4):
                        scores(q, plan, i, 1, kv, masked)
                if s1:
                    ctx_transpose(i, plan, 0)
                    ctx_transpose(i, plan, 1)
                    energy(i, plan, 1, 2)
                    energy(i, plan, 1, 3)
                if s2:
                    scores(q, plan, i, 1, 4, masked)
                    scores(q, plan, i, 1, 5, masked)
                    if s1:
                        out_project(q, plan, i, 0)
                    scores(q, plan, i, 1, 6, masked)
                    scores(q, plan, i, 1, 7, masked)
                if s1:
                    if isinstance(i, int) and i == 0:
                        pe.wait_ge(wkv_ready, 1)
                    kv_project(i, plan, "k", 0, "k_ps")
                    kv_project(i, plan, "v", 1, "v_ps")
                if s2:
                    denominators(q, 1)
                if s0:
                    z_project(i, plan, 0)
                    z_project(i, plan, 1)
                if s2:
                    values(q, 1)
                    if not s1:
                        out_project(q, plan, i, 0)
                if s1:
                    v_transpose(i, plan, 0)
                    v_transpose(i, plan, 1)
                    for j in range(2):
                        attend(i, plan, j, 0)
                        attend(i, plan, j, 1)
                if s2:
                    out_project(q, plan, i, 1)

            iteration(-1, START, True, False, False, False)
            pe.wait_ge(cw_ready, 1)
            iteration(0, FIRST, True, True, False, False)
            pe.wait_ge(flag_marks, 1)
            mm(den[0:1, 0:1], flag_col[:, 0:1], ones_eo[:, 0, 0:1], start=True, stop=False)
            mm(den[0:1, 0:1], flag_col[:, 1:2], ones_eo[:, 0, 0:1], start=False, stop=True).then_inc(flag_ps, 1)
            pe.wait_ge(wq_ready, 1)
            pe.wait_ge(flag_ready, 1)
            any_mask = pe.value_load(flag_i[0:1, 0:1], min_val=0, max_val=1)

            def rest(masked):
                if masked:
                    pe.wait_ge(mask_in, 16)
                iteration(1, SECOND, True, True, True, masked)
                with pe.Fori(2, PAIRS - 1) as i:
                    if masked:
                        pe.wait_ge(mask_in, i * 16)
                    iteration(i, FULL, True, True, True, masked)
                if masked:
                    pe.wait_ge(mask_in, (PAIRS - 1) * 16)
                iteration(PAIRS - 1, NEXT_TO_LAST, False, True, True, masked)
                if masked:
                    pe.wait_ge(mask_in, PAIRS * 16)
                iteration(PAIRS, LAST, False, False, True, masked)

            with pe.If(any_mask > 0):
                rest(True)
            with pe.Else():
                rest(False)

        @block.scalar
        def _(act):
            ident_f, copy_f, exp_f = ACT.Identity, ACT.Copy, ACT.Exp

            def z_high(i, plan, j):
                wait(act, "z_ps", i + 1, j)
                wait(act, "en_ps", i, 4 * j + 3)
                nc.scalar.activation(zh[:, j], gen[:, slot(plan, f"z{j}")], copy_f).then_inc(sem["zh_done"], 1)

            def exp_energy(i, plan, j, n):
                wait(act, "negmax_done", i, 4 * j + n)
                wait(act, "b_ps", i - 1, 2 * j + 1)
                nc.scalar.activation(att[:, j, n], wide[:, slot(plan, f"en{j}{n}")], exp_f,
                                     bias=negmax[:, j, n:n + 1], accum_out=rowsum[:, j, n:n + 1]
                                     ).then_inc(sem["exp_done"], 1)

            def tva_raw(i, plan, j, k):
                wait(act, "tva_ps", i, 4 * j + k)
                wait(act, "b_ps", i - 1, 2 * j + 1)
                wait(act, "x2_done", i - 1, j)
                nc.scalar.activation(ta[:, j, k], wide[:, slot(plan, f"tva{j}{k}"), 0:CW], copy_f
                                     ).then_inc(sem["ta_raw"], 1)

            def ctx_high(i, plan, j):
                wait(act, "et_ps", i, j)
                wait(act, "q_ps", i - 1, 3)
                nc.scalar.activation(eth[:, :, j], gen[:, slot(plan, f"et{j}")].rearrange("p (k s) -> p k s", k=KC),
                                     copy_f).then_inc(sem["eth_done"], 1)

            def k_high(i, plan):
                wait(act, "k_ps", i, 0)
                wait(act, "kb_done", i - 1, 1)
                nc.scalar.activation(kh[:], gen[:, slot(plan, "k"), 0:2 * P].rearrange("p (j s) -> p j s", j=2),
                                     ident_f, bias=bk_s).then_inc(sem["kh_done"], 1)

            def v_biased(i, plan):
                wait(act, "v_ps", i, 0)
                wait(act, "vt_ps", i - 1, 1)
                nc.scalar.activation(vts[:], gen[:, slot(plan, "v"), 0:2 * P].rearrange("p (j s) -> p j s", j=2),
                                     ident_f, bias=bv_s).then_inc(sem["vts_done"], 1)

            def v_place(i, plan, j):
                wait(act, "vt_ps", i, j)
                wait(act, "o_ps", i - 1, 1)
                src = gen[:, slot(plan, f"vt{j}"), 0:P].rearrange("p (k o d) -> p k o d", o=2, d=HD)
                dst = v2[:, j].rearrange("p (k o) c -> p k o c", o=2)
                for odd in range(2):
                    nc.scalar.activation(dst[:, :, odd, HD * odd:HD * odd + HD], src[:, :, odd], copy_f
                                         ).then_inc(sem["v2_done"], 1)

            def x2_high(i, j):
                wait(act, "x2_done", i, j)
                wait(act, "v_ps", i, 0)
                nc.scalar.activation(x2h[:, :, j], x2[:, :, j], copy_f).then_inc(sem["x2h_done"], 1)

            def q_high(q, plan, g):
                wait(act, "q_ps", q, g)
                wait(act, "st_ps", q - 1, 15)
                nc.scalar.activation(qh[:, :, g], gen[:, slot(plan, f"q{g}"), 0:2 * P].rearrange("p (j l) -> p j l", j=2),
                                     ident_f, bias=bq_s[:, g:g + 1]).then_inc(sem["qh_done"], 1)

            def residual(q, plan, j):
                wait(act, "r_ps", q, j)
                wait(act, "nrm_done", q - 1, j)
                nc.scalar.activation(res[:, j], gen[:, slot(plan, f"r{j}")], copy_f).then_inc(sem["xr_done"], 1)

            def exp_scores(q, plan, j, kv):
                wait(act, "st_ps", q, 8 * j + kv)
                if kv == 0:
                    wait(act, "o_ps", q, j - 1)
                    if isinstance(q, int) and q == 0 and j == 0:
                        act.wait_ge(wo_ready, 1)
                nc.scalar.activation(prob[:, kv], wide[:, slot(plan, f"st{j}{kv}")], exp_f
                                     ).then_inc(sem["prob_done"], 1)

            def at_high(q, j):
                wait(act, "at_done", q, j)
                wait(act, "wo_ps", q, j - 1)
                nc.scalar.activation(ath[:], at[:].rearrange("p (g l) -> p g l", g=G), copy_f
                                     ).then_inc(sem["ath_done"], 1)

            def normalise(q, j):
                wait(act, "ln_step", q, 12)
                store_before = q * 16
                if not isinstance(store_before, int) or store_before > 0:
                    act.wait_ge(out_sem[j], store_before)
                nc.scalar.activation(outb[:, j], res[:, j], ident_f, bias=nv[:, 7, j:j + 1], scale=nv[:, 6, j:j + 1]
                                     ).then_inc(sem["nrm_done"], 1)

            def sum_masks(half):
                act.wait_ge(allmask_in, 16)
                part = all_masks[:, half * B * P // 2:(half + 1) * B * P // 2]
                nc.scalar.activation(part, part, ACT.Abs, accum_out=mask_sums[:, half:half + 1]
                                     ).then_inc(mask_sums_done, 1)

            def iteration(i, plan, s0, s1, s2, s3, setup=False):
                q = i - 1
                if s2:
                    x2_high(q, 1)
                if s1:
                    for k in range(KC):
                        tva_raw(i, plan, 0, k)
                for n in range(3):
                    if s2:
                        q_high(q, plan, n)
                    if s1:
                        exp_energy(i, plan, 0, n)
                if s2:
                    q_high(q, plan, 3)
                if s1:
                    for k in range(KC):
                        tva_raw(i, plan, 1, k)
                if s3:
                    normalise(i - 2, 0)
                    if s1 or s2:
                        normalise(i - 2, 1)
                if s1:
                    exp_energy(i, plan, 0, 3)
                if s2:
                    residual(q, plan, 0)
                if s1:
                    exp_energy(i, plan, 1, 0)
                if s2:
                    exp_scores(q, plan, 0, 0)
                    residual(q, plan, 1)
                    for kv in range(1, KV):
                        exp_scores(q, plan, 0, kv)
                if s1:
                    exp_energy(i, plan, 1, 1)
                if s2:
                    for kv in range(4):
                        exp_scores(q, plan, 1, kv)
                if s1:
                    ctx_high(i, plan, 0)
                if s2 and s1:
                    at_high(q, 0)
                if s1:
                    ctx_high(i, plan, 1)
                if s2:
                    exp_scores(q, plan, 1, 4)
                    exp_scores(q, plan, 1, 5)
                if s1:
                    exp_energy(i, plan, 1, 2)
                    exp_energy(i, plan, 1, 3)
                if s2:
                    exp_scores(q, plan, 1, 6)
                    exp_scores(q, plan, 1, 7)
                if s2 and not s1:
                    at_high(q, 0)
                if setup:
                    sum_masks(0)
                if s1:
                    k_high(i, plan)
                    v_biased(i, plan)
                if s0:
                    z_high(i, plan, 0)
                    z_high(i, plan, 1)
                if s1:
                    v_place(i, plan, 0)
                    v_place(i, plan, 1)
                if setup:
                    act.wait_ge(wq_in, 16)
                    nc.scalar.activation(wq_h[:].rearrange("p k g c -> p k (g c)"), stage_w, copy_f, scale=SCALE
                                         ).then_inc(wq_high, 1)
                    sum_masks(1)
                    act.wait_ge(wo_in, 16)
                    nc.scalar.activation(wo_h[:], stage_o, copy_f).then_inc(wo_high, 1)
                if s2:
                    at_high(q, 1)
                if s1:
                    x2_high(i, 0)

            act.wait_ge(w0_in, 16 * 4)
            act.wait_ge(zeros_ready, 1)
            iteration(-1, START, True, False, False, False)
            iteration(0, FIRST, True, True, False, False, setup=True)
            iteration(1, SECOND, True, True, True, False)
            iteration(2, FULL, True, True, True, True)
            with act.Fori(3, PAIRS - 1) as i:
                iteration(i, FULL, True, True, True, True)
            iteration(PAIRS - 1, NEXT_TO_LAST, False, True, True, True)
            iteration(PAIRS, LAST, False, False, True, True)
            iteration(PAIRS + 1, None, False, False, False, True)

        @block.vector
        def _(dve):
            tt, stt, cp = nc.vector.tensor_tensor, nc.vector.scalar_tensor_tensor, nc.vector.tensor_copy

            nc.vector.memset(cw_s[:, ONE:A0], 0.0)
            nc.vector.memset(cb_s[:, ONE:ONE + 1], 1.0)
            nc.vector.memset(cb_s[:, ONE + 1:ONE + 2], 0.0)
            nc.vector.memset(cb_s[:, X0:CW], 0.0)
            dve.wait_ge(setup_pe, 1)
            cp(gram_h[:], gen[:, 0, 0:P]).then_inc(setup_dve, 1)
            cp(wtT_s, den[:, 0:P]).then_inc(setup_dve, 1)
            dve.wait_ge(setup_dve, 1)
            tt(gram_l[:], gen[:, 0, 0:P], gram_h[:].bitcast(F32), ALU.subtract).then_inc(setup_dve, 1)
            dve.wait_ge(cst_in, 16)
            cp(cw_s[:, X0:CW], ident)
            cp(cw_s[:, A0:X0], den[:, 0:P])
            dve.wait_ge(setup_pe, 2)
            cp(cb_s[:, 0:P], outt[:, 0:P])
            cp(cw_s[:, 0:P], wide[:, 0, 0:P]).then_inc(setup_dve, 1)
            dve.wait_ge(setup_dve, 4)
            cp(cw_h[:], cw_s).then_inc(setup_dve, 1)
            dve.wait_ge(setup_dve, 5)
            tt(cw_l[:], cw_s, cw_h[:].bitcast(F32), ALU.subtract).then_inc(cw_ready, 1)

            def setup_kv_weights():
                cp(sel[:], sel_f)
                cp(ident_r[:], ident)
                cp(kstack[96:96 + MROWS, 1].rearrange("m (p o) s -> m p o s", o=2),
                   row_parity.unsqueeze(1).unsqueeze(3).broadcast_to([MROWS, KV // 2, 2, P]))
                dve.wait_ge(wkv_in, 16 * 2)
                cp(wkv_h[:], stage_kv).then_inc(wkv_high, 1)
                dve.wait_ge(wkv_high, 1)
                tt(wkv_l[:], stage_kv, wkv_h[:].bitcast(F32), ALU.subtract).then_inc(wkv_ready, 1)

            def setup_query_weights():
                dve.wait_ge(w0_in, 16 * 4)
                nc.vector.tensor_scalar(bq_s[:], bq_raw, SCALE, None, ALU.mult)
                dve.wait_ge(wq_high, 1)
                stt(wq_l[:].rearrange("p k g c -> p k (g c)"), stage_w, SCALE,
                    wq_h[:].bitcast(F32).rearrange("p k g c -> p k (g c)"), ALU.mult, ALU.subtract
                    ).then_inc(wq_ready, 1)

            def setup_flag_marks():
                dve.wait_ge(mask_sums_done, 2)
                nc.vector.tensor_scalar(flag_col[:], mask_sums[:], 0.0, None, ALU.not_equal).then_inc(flag_marks, 1)

            def setup_flag_value():
                dve.wait_ge(flag_ps, 1)
                nc.vector.tensor_scalar(flag_i[:], den[0:1, 0:1], 1.0, None, ALU.min).then_inc(flag_ready, 1)

            def z_low(i, plan, j):
                wait(dve, "zh_done", i + 1, j)
                wait(dve, "en_ps", i, 4 * j + 3)
                tt(zl[:, j], gen[:, slot(plan, f"z{j}")], zh[:, j].bitcast(F32), ALU.subtract
                   ).then_inc(sem["zl_done"], 1)

            def energy_max(i, plan, j, n):
                wait(dve, "en_ps", i, 4 * j + n)
                wait(dve, "exp_done", i - 1, 4 * j + n)
                nc.vector.tensor_reduce(negmax[:, j, n:n + 1], wide[:, slot(plan, f"en{j}{n}")],
                                        AX.X, ALU.max, negate=True).then_inc(sem["negmax_done"], 1)

            def row_inverse(i, j):
                wait(dve, "exp_done", i, 4 * j + 3)
                wait(dve, "tv_done", i - 1, j)
                nc.vector.reciprocal(rowinv[:, j], rowsum[:, j]).then_inc(sem["rowinv_done"], 1)

            def layer0_out(i, plan, j):
                wait(dve, "b_ps", i, 2 * j + 1)
                first, second = slot(plan, f"b{j}0"), slot(plan, f"b{j}1")
                assert second == first + 1
                att_v = wide[:, first:first + 2].rearrange("p a (b c) -> p (a b) c", b=2)
                nc.vector.tensor_scalar(colneg[:, j], att_v[:, :, ONE], -1.0, -COL_EPS, ALU.mult, ALU.add
                                        ).then_inc(sem["colneg_done"], 1)
                wait(dve, "colneg_done", i, j)
                nc.vector.reciprocal(colinv[:, j], colneg[:, j]).then_inc(sem["colinv_done"], 1)
                wait(dve, "colinv_done", i, j)
                for m in range(KC):
                    stt(ta[:, j, m, A0:A0 + P], att_v[:, m, 0:P], colinv[:, j, m:m + 1], ta[:, j, m, A0:A0 + P],
                        ALU.mult, ALU.add).then_inc(sem["pre_done"], 1)
                wait(dve, "pre_done", i, 4 * j + 3)
                wait(dve, "x2l_done", i - 1, j)
                wait(dve, "r_ps", i - 1, j)
                stt(x2[:, :, j], ta[:, j, :, A0:A0 + P], 0.0, ta[:, j, :, X0:CW], ALU.max, ALU.add
                    ).then_inc(sem["x2_done"], 1)

            def x2_low(i, j):
                wait(dve, "x2h_done", i, j)
                wait(dve, "v_ps", i, 0)
                tt(x2l[:, :, j], x2[:, :, j], x2h[:, :, j].bitcast(F32), ALU.subtract).then_inc(sem["x2l_done"], 1)

            def ctx_low(i, plan, j):
                wait(dve, "eth_done", i, j)
                wait(dve, "q_ps", i - 1, 3)
                tt(etl[:, :, j], gen[:, slot(plan, f"et{j}")].rearrange("p (k s) -> p k s", k=KC),
                   eth[:, :, j].bitcast(F32), ALU.subtract).then_inc(sem["etl_done"], 1)

            def k_low(i, plan):
                wait(dve, "kh_done", i, 0)
                wait(dve, "kp_done", i - 1, 0)
                stt(kl[:], gen[:, slot(plan, "k"), 0:2 * P].rearrange("p (j s) -> p j s", j=2), bk_s,
                    kh[:].bitcast(F32), ALU.add, ALU.subtract).then_inc(sem["kl_done"], 1)

            def q_low(q, plan, g):
                wait(dve, "qh_done", q, g)
                wait(dve, "st_ps", q - 1, 15)
                stt(ql[:, :, g], gen[:, slot(plan, f"q{g}"), 0:2 * P].rearrange("p (j l) -> p j l", j=2),
                    bq_s[:, g:g + 1], qh[:, :, g].bitcast(F32), ALU.add, ALU.subtract).then_inc(sem["ql_done"], 1)

            def score_max(q, plan, j, g, half):
                wait(dve, "mx_ps", q, 8 * j + 2 * g + half)
                if g == 0 and half == 0:
                    wait(dve, "mrow_done", q - 1, 2 * j + 1)
                at_head = g * KV + 4 * half
                nc.vector.tensor_reduce(maxima[:, j, at_head:at_head + 4],
                                        wide[:, slot(plan, f"mx{j}{g}{half}")].rearrange("p (b s) -> p b s", s=P),
                                        AX.X, ALU.max, negate=True).then_inc(sem["max_done"], 1)

            def max_split(q, j):
                wait(dve, "max_done", q, 8 * j + 7)
                wait(dve, "m_ps", q - 1, j)
                heads = maxima[:, j].rearrange("x (g p o) -> x p g o", g=G, o=2)
                high, low = (mrow[:, j, :, part].rearrange("x p (g o) -> x p g o", g=G) for part in range(2))
                cp(high, heads).then_inc(sem["mrow_done"], 1)
                wait(dve, "mrow_done", q, 2 * j)
                tt(low, heads, high.bitcast(F32), ALU.subtract).then_inc(sem["mrow_done"], 1)

            def max_rows(q, plan, j):
                wait(dve, "m_ps", q, j)
                wait(dve, "st_ps", q, 8 * j - 1)
                tt(mrep[:], gen[0:64, slot(plan, f"m{j}")].rearrange("p (g l) -> p g l", g=G),
                   gmask.unsqueeze(2).broadcast_to([64, G, P]), ALU.mult).then_inc(sem["mrep_done"], 1)

            def inverse_denominators(q, j):
                wait(dve, "den_ps", q, j)
                wait(dve, "atl_done", q + j - 1, 1 - j)
                nc.vector.reciprocal(at[:], den[:]).then_inc(sem["dinv_done"], 1)

            def weigh_out(q, j):
                wait(dve, "dinv_done", q, j)
                wait(dve, "o_ps", q, j)
                tt(at[:], outt[:], at[:], ALU.mult).then_inc(sem["at_done"], 1)

            def at_low(q, j):
                wait(dve, "ath_done", q, j)
                wait(dve, "wo_ps", q, j - 1)
                tt(atl[:], at[:].rearrange("p (g l) -> p g l", g=G), ath[:].bitcast(F32), ALU.subtract
                   ).then_inc(sem["atl_done"], 1)

            def residual_add(q, plan, j):
                wait(dve, "wo_ps", q, j)
                wait(dve, "xrb_done", q, j)
                tt(res[:, j], gen[:, slot(plan, f"wo{j}")], res[:, j], ALU.add).then_inc(sem["res_done"], 1)

            def row_statistics(q, j):
                wait(dve, "res_done", q, j)
                wait(dve, "ln_var", q - 1, 5)
                nc.vector.bn_stats(bns[:, j], res[:, j]).then_inc(sem["bns_done"], 1)

            def root_guess(q):
                wait(dve, "ln_var", q, 5)
                nc.vector.tensor_scalar(yi[:], nv[:, 0].bitcast(I32), -0.5, 1597463007.0, ALU.mult, ALU.add
                                        ).then_inc(sem["ln_guess"], 1)

            def finish_last_rows():
                q = PAIRS - 1
                wait(dve, "ln_step", q, 12)
                dve.wait_ge(out_sem[1], q * 16)
                nc.vector.tensor_scalar(outb[:, 1], res[:, 1], nv[:, 6, 1:2], nv[:, 7, 1:2], ALU.mult, ALU.add
                                        ).then_inc(last_rows, 1)
                dve.wait_ge(last_rows, 1)
                tt(outb[:, 1], outb[:, 1], gamma_b[:], ALU.mult).then_inc(last_rows, 1)
                dve.wait_ge(last_rows, 2)
                tt(outb[:, 1], outb[:, 1], beta_b[:], ALU.add).then_inc(last_rows, 1)

            def iteration(i, plan, s0, s1, s2, s3, setup=False):
                q = i - 1

                def both_score_max(g):
                    score_max(q, plan, 0, g, 0)
                    score_max(q, plan, 0, g, 1)

                if s2:
                    x2_low(q, 1)
                if s3:
                    residual_add(i - 2, FULL, 1)
                    row_statistics(i - 2, 1)
                for n in range(3):
                    if s2:
                        q_low(q, plan, n)
                    if s1:
                        energy_max(i, plan, 0, n)
                    if s3 and n == 0:
                        root_guess(i - 2)
                    if s2 and n > 0:
                        both_score_max(n - 1)
                if s2:
                    q_low(q, plan, 3)
                    both_score_max(2)
                    both_score_max(3)
                    max_split(q, 0)
                if s1:
                    energy_max(i, plan, 0, 3)
                if s2:
                    max_rows(q, plan, 0)
                if s1:
                    energy_max(i, plan, 1, 0)
                if s1:
                    row_inverse(i, 0)
                if s2:
                    for kv in range(KV):
                        score_max(q, plan, 1, kv // 2, kv % 2)
                    max_split(q, 1)
                if s1:
                    energy_max(i, plan, 1, 1)
                if s2:
                    max_rows(q, plan, 1)
                if s2:
                    inverse_denominators(q, 0)
                    weigh_out(q, 0)
                if s1:
                    ctx_low(i, plan, 0)
                if s2:
                    at_low(q, 0)
                if s1:
                    energy_max(i, plan, 1, 2)
                    energy_max(i, plan, 1, 3)
                    ctx_low(i, plan, 1)
                    row_inverse(i, 1)
                if s2 and s1:
                    residual_add(q, plan, 0)
                    row_statistics(q, 0)
                if s1:
                    k_low(i, plan)
                if s0:
                    z_low(i, plan, 0)
                    z_low(i, plan, 1)
                if setup:
                    setup_query_weights()
                    setup_flag_marks()
                if s2:
                    inverse_denominators(q, 1)
                    weigh_out(q, 1)
                    at_low(q, 1)
                if s2 and not s1:
                    residual_add(q, plan, 0)
                    row_statistics(q, 0)
                if s1:
                    layer0_out(i, plan, 0)
                    layer0_out(i, plan, 1)
                    x2_low(i, 0)

            iteration(-1, START, True, False, False, False)
            setup_kv_weights()
            iteration(0, FIRST, True, True, False, False, setup=True)
            setup_flag_value()
            iteration(1, SECOND, True, True, True, False)
            iteration(2, FULL, True, True, True, True)
            with dve.Fori(3, PAIRS - 1) as i:
                iteration(i, FULL, True, True, True, True)
            iteration(PAIRS - 1, NEXT_TO_LAST, False, True, True, True)
            iteration(PAIRS, LAST, False, False, True, True)
            iteration(PAIRS + 1, None, False, False, False, True)
            finish_last_rows()


def shape_constants():
    c = np.zeros((P, C_ALL), np.float32)
    c[:, C_ID:C_ID + P] = np.eye(P)
    for k in range(KV):
        c[HD * k:HD * (k + 1), C_KVMASK + k] = 1.0
        c[HD * k:HD * (k + 1), C_ODD + k % 2] = 1.0
    ones = c[:, C_ONES:C_ONES + 4 * HD].reshape(P, 2, 2 * HD)
    ones[:, 0, :HD] = 1.0
    ones[:, 1, HD:] = 1.0
    c[:, C_ONES:C_ONES + 4 * HD] = ones.reshape(P, -1)
    for pair in range(KV // 2):
        for part in range(2):
            for g in range(G):
                for odd in range(2):
                    row = (part * G + g) * 2 + odd
                    c[pair * MROWS + row, C_GMASK + g] = 1.0
                    c[pair * MROWS + row, C_SEL + 2 * pair + odd] = 1.0
                    c[3 * 32 + row, C_MODD + odd] = 1.0
    c[:, C_LN:C_ALL] = LN_CONSTANTS
    return c


def kernel(x, ctx_2048, mask_Bx1xSxS2_ff0, L0_xattn_w_qk, L0_xattn_w_v, L0_xattn_b_v, L0_xattn_w_t, L0_xattn_b_t,
           L1_xattn_Wq, L1_xattn_bq, L1_xattn_Wk, L1_xattn_bk, L1_xattn_Wv, L1_xattn_bv, L1_xattn_Wo, L1_xattn_bo,
           L1_xattn_gamma, L1_xattn_beta):
    import concourse.bacc as bacc
    from concourse.bass_utils import run_bass_kernel_spmd

    wq = np.asarray(L1_xattn_Wq).reshape(N, KV, G, HD).transpose(0, 2, 1, 3).reshape(N, N)
    wo = np.asarray(L1_xattn_Wo).reshape(KV, G, HD, N).transpose(1, 0, 2, 3).reshape(N, N)
    bq = np.asarray(L1_xattn_bq).reshape(KV, G, HD).transpose(0, 2, 1).reshape(P, G)
    columns = np.concatenate([bq] + [np.asarray(b).reshape(P, 1) for b in (L1_xattn_bk, L1_xattn_bv, L0_xattn_b_v)], 1)
    arrays = {
        "in_x": x, "in_ctx": ctx_2048, "in_mask": mask_Bx1xSxS2_ff0, "in_w_qk": L0_xattn_w_qk, "in_w_v": L0_xattn_w_v,
        "in_w_t": L0_xattn_w_t, "in_b_t": L0_xattn_b_t, "in_Wq": wq, "in_Wk": L1_xattn_Wk, "in_Wv": L1_xattn_Wv,
        "in_Wo": wo, "in_bo": L1_xattn_bo, "in_gamma": L1_xattn_gamma, "in_beta": L1_xattn_beta,
        "in_columns": columns, "shape_constants": shape_constants(),
    }
    arrays = {n: np.ascontiguousarray(a) for n, a in arrays.items()}
    nc = bacc.Bacc("TRN2", target_bir_lowering=False, num_devices=1)
    args = [nc.dram_tensor(n, a.shape, mybir.dt.from_np(a.dtype), kind="ExternalInput").ap() for n, a in arrays.items()]
    out = nc.dram_tensor("out_x", (B, P, N), F32, kind="ExternalOutput").ap()
    build_xattn(nc, *args, out)
    r = run_bass_kernel_spmd(nc, [arrays], core_ids=[0])
    return r.results[0]["out_x"]
```
